# Optimizing a Trainium2 kernel written in Bass

```python
import numpy as np
import jax
import jax.numpy as jnp

def _softmax(x, axis=-1):
    return jax.nn.softmax(x, axis=axis)

def _gelu(x):
    return jax.nn.gelu(x, approximate=True)

def _silu(x):
    return jax.nn.silu(x)

def _sigmoid(x):
    return jax.nn.sigmoid(x)

def _layernorm(x, axis=-1, eps=1e-05):
    m = jnp.mean(x, axis=axis, keepdims=True)
    v = jnp.var(x, axis=axis, keepdims=True)
    return (x - m) / jnp.sqrt(v + eps)

def _scatter_add(tgt, idx, src, axis=0):
    return tgt.at[idx].add(src)

def _segment_sum(src, seg, n):
    return jax.ops.segment_sum(src, seg, n)
kernel_name = 'mk_adaln_ffn_d1_seqx_r8_947eaa'

def setup_inputs(seed: int=0):
    np.random.seed(seed)
    _w = jnp.asarray

    def _rec_inputs():
        import jax
        import jax.numpy as jnp
        _rk = jax.random.key(seed)
        x = -0.000125 + 0.9999 * jax.random.normal(jax.random.fold_in(_rk, 1), (128, 32, 512), jnp.float32)
        _lenS = 32 - jax.random.randint(jax.random.fold_in(_rk, 7), (128,), 0, max(1, 32 // 4) + 1, jnp.int32)
        _lenS2 = 32 - jax.random.randint(jax.random.fold_in(_rk, 8), (128,), 0, max(1, 32 // 4) + 1, jnp.int32)
        cond_128 = 0.0061147 + 1.02565 * jax.random.normal(jax.random.fold_in(_rk, 11), (128, 128), jnp.float32)
        return (x, cond_128)
    x, cond_128 = _rec_inputs()

    def _L0_cond_setup():
        import jax, jax.numpy as jnp
        import numpy as np
        K = 8
        T = 1.0
        D_EMBD = 128
        IN_C = 32
        OUT_C = 32
        BS = 32
        H = 512
        HID = 128
        key = jax.random.key(seed)
        ks = jax.random.split(key, 10)
        s = lambda fan_in: 1.0 / np.sqrt(fan_in)
        return {'x': jax.random.normal(ks[0], (BS, IN_C, H), dtype=jnp.float32), 'embedding': jax.random.normal(ks[1], (BS, D_EMBD), dtype=jnp.float32), 'W0': jax.random.normal(ks[2], (D_EMBD, HID), dtype=jnp.float32) * s(D_EMBD), 'b0': jnp.zeros((HID,), dtype=jnp.float32), 'W1': jax.random.normal(ks[3], (HID, HID), dtype=jnp.float32) * s(HID), 'b1': jnp.zeros((HID,), dtype=jnp.float32), 'W2': jax.random.normal(ks[4], (HID, K), dtype=jnp.float32) * s(HID), 'b2': jnp.zeros((K,), dtype=jnp.float32), 'weight': jax.random.normal(ks[5], (K, OUT_C, IN_C, 1), dtype=jnp.float32) * s(IN_C), 'bias_k': jax.random.normal(ks[6], (K, OUT_C), dtype=jnp.float32) * 0.1}
    _L0_cond_all = _L0_cond_setup()
    _L0_cond_in = {k: v for k, v in _L0_cond_all.items() if k in ('W0', 'b0', 'W1', 'b1', 'W2', 'b2', 'weight', 'bias_k')}
    del _L0_cond_all

    def _L0_ffn_setup():
        import jax, jax.numpy as jnp
        import numpy as np
        B, S, D, O, R, E = (4, 256, 512, 512, 16, 8)
        SCALING = 32.0 / 16.0
        key = jax.random.key(seed)
        ks = jax.random.split(key, 7)
        x = jax.random.normal(ks[0], (B, S, D), dtype=jnp.float32)
        W_base = jax.random.normal(ks[1], (O, D), dtype=jnp.float32) * 0.02
        b_base = jnp.zeros((O,), dtype=jnp.float32)
        A_w = jax.random.normal(ks[2], (R, D), dtype=jnp.float32) * 0.02
        B_w = jax.random.normal(ks[3], (O, R), dtype=jnp.float32) * 0.02
        router_w = jax.random.normal(ks[4], (E, D), dtype=jnp.float32) * 0.02
        cores = jax.random.normal(ks[5], (E, R, R), dtype=jnp.float32)
        return {'x': x, 'W_base': W_base, 'b_base': b_base, 'A_w': A_w, 'B_w': B_w, 'router_w': router_w, 'cores': cores}
    _L0_ffn_all = _L0_ffn_setup()
    _L0_ffn_in = {k: v for k, v in _L0_ffn_all.items() if k in ('W_base', 'b_base', 'A_w', 'B_w', 'router_w', 'cores')}
    del _L0_ffn_all
    return {'x': x, 'cond_128': cond_128, 'L0_cond_W0': _L0_cond_in['W0'], 'L0_cond_b0': _L0_cond_in['b0'], 'L0_cond_W1': _L0_cond_in['W1'], 'L0_cond_b1': _L0_cond_in['b1'], 'L0_cond_W2': _L0_cond_in['W2'], 'L0_cond_b2': _L0_cond_in['b2'], 'L0_cond_weight': _L0_cond_in['weight'], 'L0_cond_bias_k': _L0_cond_in['bias_k'], 'L0_ffn_W_base': _L0_ffn_in['W_base'], 'L0_ffn_b_base': _L0_ffn_in['b_base'], 'L0_ffn_A_w': _L0_ffn_in['A_w'], 'L0_ffn_B_w': _L0_ffn_in['B_w'], 'L0_ffn_router_w': _L0_ffn_in['router_w'], 'L0_ffn_cores': _L0_ffn_in['cores']}

def reference(x, cond_128, L0_cond_W0, L0_cond_b0, L0_cond_W1, L0_cond_b1, L0_cond_W2, L0_cond_b2, L0_cond_weight, L0_cond_bias_k, L0_ffn_W_base, L0_ffn_b_base, L0_ffn_A_w, L0_ffn_B_w, L0_ffn_router_w, L0_ffn_cores):
    import jax
    import jax.numpy as jnp

    def _L0_cond_ref(x, embedding, W0, b0, W1, b1, W2, b2, weight, bias_k):
        import jax, jax.numpy as jnp
        import numpy as np
        K = 8
        T = 1.0
        D_EMBD = 128
        IN_C = 32
        OUT_C = 32
        BS = 32
        H = 512
        HID = 128
        h = jax.nn.gelu(embedding @ W0 + b0, approximate=False)
        h = jax.nn.gelu(h @ W1 + b1, approximate=False)
        att = jax.nn.softmax((h @ W2 + b2) / T, axis=-1)
        agg_w = jnp.einsum('bk,koi->boi', att, weight[..., 0])
        agg_b = att @ bias_k
        out = jnp.einsum('boi,bih->boh', agg_w, x) + agg_b[:, :, None]
        return out

    def _L0_ffn_ref(x, W_base, b_base, A_w, B_w, router_w, cores):
        import jax, jax.numpy as jnp
        import numpy as np
        B, S, D, O, R, E = (4, 256, 512, 512, 16, 8)
        SCALING = 32.0 / 16.0
        result = jnp.einsum('bsd,od->bso', x, W_base) + b_base
        ax = jnp.einsum('bsd,rd->bsr', x, A_w)
        probs = jax.nn.softmax(jnp.einsum('bsd,ed->bse', x, router_w), axis=-1)
        per_expert = jnp.einsum('bsr,erq->bseq', ax, cores)
        mixed = jnp.einsum('bseq,bse->bsq', per_expert, probs)
        result = result + jnp.einsum('bsr,or->bso', mixed, B_w) * SCALING
        return result
    x = x + _L0_ffn_ref(_L0_cond_ref(x, cond_128, L0_cond_W0, L0_cond_b0, L0_cond_W1, L0_cond_b1, L0_cond_W2, L0_cond_b2, L0_cond_weight, L0_cond_bias_k), L0_ffn_W_base, L0_ffn_b_base, L0_ffn_A_w, L0_ffn_B_w, L0_ffn_router_w, L0_ffn_cores)
    return x

_drawn_inputs = setup_inputs


def setup_inputs(seed=0):
    import zlib

    import numpy as np

    out = dict(_drawn_inputs(seed))
    spreads = {'L0_cond_b0': (0.0, 0.8),
     'L0_cond_b1': (0.0, 0.683),
     'L0_cond_b2': (0.0, 0.648),
     'L0_ffn_b_base': (0.0, 0.1)}
    factors = {'L0_cond_bias_k': 3.347, 'L0_ffn_router_w': 8.0}
    for name, (base, spread) in spreads.items():
        noise = np.random.default_rng([zlib.crc32(name.encode()), seed]).standard_normal(out[name].shape)
        drawn = base * np.exp(spread * noise) if base else spread * noise
        out[name] = jnp.asarray(drawn.astype(out[name].dtype))
    for name, factor in factors.items():
        out[name] = (out[name] * factor).astype(out[name].dtype)
    return out
```

```python
from contextlib import ExitStack

import concourse.bass as bass
from concourse import mybir

F32 = mybir.dt.float32
F32R = mybir.dt.float32r
ALU = mybir.AluOpType
ACT = mybir.ActivationFunctionType
AX_X = mybir.AxisListType.X

P = 128
GROUP = 4


def adaln_ffn(nc, x, cond, W0, b0, W1, b1, W2, b2, weight, bias_k, W_base, b_base, A_w, B_w,
              router_w, cores, out):
    BATCH, CH, D = x.shape
    KC = W2.shape[1]
    O = W_base.shape[0]
    E, R, _ = cores.shape
    SPT = P // CH
    TILES = BATCH * CH // P
    GROUPS = TILES // GROUP
    DC = D // P
    OH = O // 2
    SM = R + E
    SH = SM // 2
    HC = OH + SH
    SCALING = 2.0
    IH = CH // 2
    assert E * R == P and O % 2 == 0 and D % P == 0 and TILES % GROUP == 0
    MID_H, MID_L, MID_H2, BIAS = 0, 32, 64, 96
    NBIAS = 5

    x_t = x.rearrange("(g j s) c d -> g j (s c) d", j=GROUP, s=SPT)
    out_t = out.rearrange("(g j s) c d -> g j (s c) d", j=GROUP, s=SPT)

    with ExitStack() as ctx:
        def sb(name, shape, dt=F32):
            return ctx.enter_context(nc.sbuf_tensor(name, shape, dt))

        def ps(name, shape):
            return ctx.enter_context(nc.psum_tensor(name, shape, F32))

        def sem(name):
            return ctx.enter_context(nc.semaphore(name))

        aggw_dram = nc.dram_tensor("aggw_scratch", (BATCH, CH * CH), F32).ap()
        aggb_dram = nc.dram_tensor("aggb_scratch", (2, BATCH, CH), F32).ap()

        ident = sb("ident", [P, P])
        ones_r = sb("ones_r", [P, P], F32R)
        samemask = sb("samemask", [P, SPT])
        cond_sb = sb("cond_sb", [P, P])
        condT = sb("condT", [P, P])
        W0_sb = sb("W0_sb", [P, P])
        W1_sb = sb("W1_sb", [P, P])
        W2_sb = sb("W2_sb", [P, KC])
        b0_col = sb("b0_col", [P, 1])
        b1_col = sb("b1_col", [P, 1])
        b2_bc = sb("b2_bc", [P, KC])
        h1T = sb("h1T", [P, P])
        h2T = sb("h2T", [P, P])
        clog = sb("clog", [P, KC])
        cnmax = sb("cnmax", [P, 1])
        cexp = sb("cexp", [P, KC])
        csum = sb("csum", [P, 1])
        crinv = sb("crinv", [P, 1])
        att = sb("att", [P, KC])
        attT = sb("attT", [KC, P])
        kw = sb("kw", [KC, CH, CH])
        kb = sb("kb", [KC, SPT, CH])
        aggw_sb = sb("aggw_sb", [P, CH, CH])
        aggb_hl = sb("aggb_hl", [P, 2, CH], F32R)
        aggw_c = sb("aggw_c", [P, TILES, CH])
        aggb_col = sb("aggb_col", [P, TILES])
        bias_rows = sb("bias_rows", [P, TILES * P])
        Wb_sb = sb("Wb_sb", [P, O // P, D])
        ar_sb = sb("ar_sb", [SM, D])
        Bw_sb = sb("Bw_sb", [P, O // P, R])
        bb_row = sb("bb_row", [1, O])
        cores_sb = sb("cores_sb", [P, R])
        WT_h = sb("WT_h", [P, DC, 2, HC], F32R)
        WT_l = sb("WT_l", [P, DC, 2, HC], F32R)
        wsum_s = sb("wsum_s", [P, SM])
        row_src = sb("row_src", [1, NBIAS, O], F32R)
        core_h = sb("core_h", [P, BIAS], F32R)
        core_l = sb("core_l", [P, BIAS], F32R)
        tail_w = sb("tail_w", [P, O], F32R)
        x_sb = sb("x_sb", [P, GROUP, D])
        xres = sb("xres", [P, GROUP, D])
        xT_h = sb("xT_h", [P, 2, DC, P], F32R)
        xT_l = sb("xT_l", [P, 2, DC, P], F32R)
        u_h = sb("u_h", [P, GROUP, 2, HC], F32R)
        u_l = sb("u_l", [P, GROUP, 2, HC], F32R)
        ablk = sb("ablk", [P, SPT, CH])
        ablk_h = sb("ablk_h", [P, 2, SPT, CH], F32R)
        ablk_l = sb("ablk_l", [P, 2, SPT, CH], F32R)
        small = sb("small", [P, SM])
        nmax = sb("nmax", [P, 1])
        eprob = sb("eprob", [P, E])
        esum = sb("esum", [P, 1])
        rinv = sb("rinv", [P, 1])
        z = sb("z", [P, E, R])
        zT_h = sb("zT_h", [P, P], F32R)
        zT_l = sb("zT_l", [P, P], F32R)
        tail_s = sb("tail_s", [P, 2, P], F32R)
        out_sb = sb("out_sb", [P, GROUP, O])

        pm = [ps("pm0", [P, 2, 512]), ps("pm1", [P, 2, 512])]
        pu = [ps("pu0", [P, 512]), ps("pu1", [P, 512])]
        px = ps("px", [P, 512])
        pz = ps("pz", [P, 512])
        pzT = pz[:, 0:P]
        pmT = pz[0:BIAS, P:2 * P]

        ld_cond, ld_w0, ld_w1, ld_w2 = sem("ld_cond"), sem("ld_w0"), sem("ld_w1"), sem("ld_w2")
        ld_b01, ld_b2, ld_kw, ld_kb = sem("ld_b01"), sem("ld_b2"), sem("ld_kw"), sem("ld_kb")
        ld_wb, ld_ar, ld_bw, ld_bb = sem("ld_wb"), sem("ld_ar"), sem("ld_bw"), sem("ld_bb")
        ld_cores = sem("ld_cores")
        ld_x = [sem(f"ld_x{j}") for j in range(GROUP)]
        x_kept = [sem(f"x_kept{j}") for j in range(GROUP)]
        stored = [sem(f"stored{j}") for j in range(GROUP)]
        scratch_out, aggw_back, rows_back = sem("scratch_out"), sem("aggw_back"), sem("rows_back")
        tail_rows = sem("tail_rows")
        consts, ident_ok, rows_set = sem("consts"), sem("ident_ok"), sem("rows_set")
        condT_ps, condT_ok = sem("condT_ps"), sem("condT_ok")
        h1_ps, h1_ok, h2_ps, h2_ok = sem("h1_ps"), sem("h1_ok"), sem("h2_ps"), sem("h2_ok")
        clog_ps, clog_ok, cnmax_ok, cexp_ok = sem("clog_ps"), sem("clog_ok"), sem("cnmax_ok"), sem("cexp_ok")
        crinv_ok, att_ok, attT_ps, attT_ok = sem("crinv_ok"), sem("att_ok"), sem("attT_ps"), sem("attT_ok")
        aggw_ps, aggw_a, aggw_d = sem("aggw_ps"), sem("aggw_a"), sem("aggw_d")
        aggb_ps, aggb_hl_ok, aggb_col_ok = sem("aggb_ps"), sem("aggb_hl_ok"), sem("aggb_col_ok")
        arT_ps, arT_h_ok, arT_l_ok = sem("arT_ps"), sem("arT_h_ok"), sem("arT_l_ok")
        wT_ps, wT_h_ok, wT_l_ok = sem("wT_ps"), sem("wT_h_ok"), sem("wT_l_ok")
        wsum_ps, row_h_ok, row_l_ok, wsum_s_ok = sem("wsum_ps"), sem("row_h_ok"), sem("row_l_ok"), sem("wsum_s_ok")
        bwT_ps, bwT_h_ok, bwT_l_ok = sem("bwT_ps"), sem("bwT_h_ok"), sem("bwT_l_ok")
        core_h_ok, core_l_ok = sem("core_h_ok"), sem("core_l_ok")
        xT_ps, xT_h_ok, xT_l_ok = sem("xT_ps"), sem("xT_h_ok"), sem("xT_l_ok")
        u_ps = [sem("u_ps0"), sem("u_ps1")]
        u_h_ok = [sem("u_h_ok0"), sem("u_h_ok1")]
        u_l_ok = [sem("u_l_ok0"), sem("u_l_ok1")]
        small_ok, nmax_ok, eprob_ok, rinv_ok, z_ok = (
            sem("small_ok"), sem("nmax_ok"), sem("eprob_ok"), sem("rinv_ok"), sem("z_ok"))
        zT_ps, zT_h_ok, zT_l_ok = sem("zT_ps"), sem("zT_h_ok"), sem("zT_l_ok")
        mT_ps, mT_h_ok, mT_l_ok = sem("mT_ps"), sem("mT_h_ok"), sem("mT_l_ok")
        ablk_f_ok, ablk_h_ok, ablk_ok, brow_ok = (
            sem("ablk_f_ok"), sem("ablk_h_ok"), sem("ablk_ok"), sem("brow_ok"))
        mix_ps = [sem("mix_ps0"), sem("mix_ps1")]
        tail_ps = [sem("tail_ps0"), sem("tail_ps1")]
        final_ok = [sem("final_ok0"), sem("final_ok1")]

        block = ctx.enter_context(nc.Block())

        def tile_of(g, j):
            return g * GROUP + j

        def nth_of_parity(g, j):
            return g * (GROUP // 2) + j // 2

        def wait_past(eng, semaphore, n):
            if not (isinstance(n, int) and n <= 0):
                eng.wait_ge(semaphore, n)

        @block.sync
        def _(sp):
            sp.dma_start(cond_sb[:], cond).then_inc(ld_cond, 16)
            sp.dma_start(W0_sb[:], W0).then_inc(ld_w0, 16)
            sp.dma_start(Wb_sb[:, 0:2, :],
                         W_base[0:2 * P, :].rearrange("(c p) d -> p c d", p=P)).then_inc(ld_wb, 16)
            sp.dma_start(x_sb[:, 0, :], x_t[0, 0]).then_inc(ld_x[0], 16)
            sp.dma_start(W1_sb[:], W1).then_inc(ld_w1, 16)
            sp.dma_start(W2_sb[:], W2).then_inc(ld_w2, 16)
            sp.dma_start(b2_bc[:], b2.unsqueeze(0).to_broadcast([P, KC])).then_inc(ld_b2, 16)
            sp.dma_start(kb[:], bias_k.unsqueeze(1).to_broadcast([KC, SPT, CH])).then_inc(ld_kb, 16)
            sp.dma_start(kw[:], weight.rearrange("k o i one -> k o (i one)")).then_inc(ld_kw, 16)
            for j in range(1, GROUP):
                sp.dma_start(x_sb[:, j, :], x_t[0, j]).then_inc(ld_x[j], 16)
            sp.dma_start(cores_sb[:], cores.rearrange("e r q -> (e r) q")).then_inc(ld_cores, 16)
            sp.dma_start(Bw_sb[:], B_w.rearrange("(c p) r -> p c r", p=P)).then_inc(ld_bw, 16)
            sp.dma_start(bb_row[:], b_base.unsqueeze(0)).then_inc(ld_bb, 16)

            def keep_x(g, j):
                sp.wait_ge(ld_x[j], 16 * (g + 1))
                sp.dma_start(xres[:, j, :], x_sb[:, j, :]).then_inc(x_kept[j], 16)

            def next_x(g, j):
                sp.wait_ge(xT_ps, tile_of(g, j) + 1)
                sp.wait_ge(x_kept[j], 16 * (g + 1))
                sp.dma_start(x_sb[:, j, :], x_t[g + 1, j]).then_inc(ld_x[j], 16)

            def store(g, j):
                sp.wait_ge(final_ok[j % 2], nth_of_parity(g, j) + 1)
                sp.dma_start(out_t[g, j], out_sb[:, j, :]).then_inc(stored[j], 16)

            for j in range(GROUP):
                keep_x(0, j)
            next_x(0, 0)
            next_x(0, 1)
            sp.wait_ge(aggw_a, 1)
            sp.wait_ge(aggw_d, 1)
            sp.dma_start(aggw_dram, aggw_sb[:].rearrange("b i o -> b (i o)")).then_inc(scratch_out, 16)
            sp.wait_ge(aggb_hl_ok, 2)
            sp.dma_start(aggb_dram.rearrange("h b o -> b h o"), aggb_hl[:].bitcast(F32)).then_inc(scratch_out, 16)
            sp.wait_ge(scratch_out, 32)
            back = aggw_dram.rearrange("(t s) (i o) -> s i t o", s=SPT, i=CH)
            for s in range(SPT):
                sp.dma_start(aggw_c[s * CH:(s + 1) * CH, :, :], back[s]).then_inc(aggw_back, 16)
            sp.wait_ge(rows_set, 1)
            for r, part in enumerate((0, 0, 1)):
                sp.dma_start(bias_rows[BIAS + r:BIAS + r + 1, :],
                             aggb_dram[part:part + 1].rearrange("h b o -> h (b o)")).then_inc(rows_back, 16)
            next_x(0, 2)
            next_x(0, 3)
            sp.wait_ge(row_h_ok, 3)
            sp.wait_ge(row_l_ok, 2)
            for r in range(NBIAS):
                sp.dma_start(tail_w[BIAS + r:BIAS + r + 1, :].bitcast(F32),
                             row_src[0:1, r, :].bitcast(F32)).then_inc(tail_rows, 16)

            def group(g, more):
                for j in range(GROUP):
                    store(g - 1, j)
                    keep_x(g, j)
                    if more:
                        next_x(g, j)

            group(1, True)
            with sp.Fori(2, GROUPS - 1) as g:
                group(g, True)
            group(GROUPS - 1, False)
            for j in range(GROUP):
                store(GROUPS - 1, j)
            for j in range(GROUP):
                sp.wait_ge(stored[j], 16 * GROUPS)

        @block.gpsimd
        def _(pool):
            pool.memset(ident[:], 0.0).then_inc(ident_ok, 1)
            pool.wait_ge(ident_ok, 1)
            pool.affine_select(out=ident[:], in_=ident[:], compare_op=ALU.not_equal, fill=1.0, base=0,
                               pattern=[[-1, P]], channel_multiplier=1).then_inc(ident_ok, 1)
            pool.wait_ge(ident_ok, 2)
            pool.memset(bias_rows[BIAS:P, :], 1.0).then_inc(rows_set, 1)
            pool.wait_ge(rows_set, 1)
            pool.wait_ge(consts, 2 + SPT)
            pool.wait_ge(aggw_back, 16 * SPT)
            pool.wait_ge(rows_back, 16 * 3)

            def mixing_matrix(g, j):
                m = tile_of(g, j)
                par = j % 2
                wait_past(pool, ablk_ok, m)
                wait_past(pool, brow_ok, m)
                wait_past(pool, mix_ps[par], nth_of_parity(g, j))
                aggw_t = aggw_c[:, bass.ds(m, 1), :].to_broadcast([P, SPT, CH])
                mask = samemask[:].unsqueeze(2).to_broadcast([P, SPT, CH])
                pool.tensor_tensor(ablk[:], aggw_t, mask, ALU.mult).then_inc(ablk_f_ok, 1)
                pool.tensor_tensor(ablk_h[:, par], aggw_t, mask, ALU.mult).then_inc(ablk_h_ok, 1)
                pool.wait_ge(ablk_f_ok, m + 1)
                pool.wait_ge(ablk_h_ok, m + 1)
                pool.tensor_tensor(ablk_l[:, par], ablk[:], ablk_h[:, par].bitcast(F32),
                                   ALU.subtract).then_inc(ablk_ok, 1)
                wait_past(pool, tail_ps[par], nth_of_parity(g, j))
                pool.wait_ge(ablk_ok, m + 1)
                pool.tensor_copy(tail_s[BIAS:P, par, :],
                                 bias_rows[BIAS:P, bass.ds(m * P, P)]).then_inc(brow_ok, 1)

            for j in range(GROUP):
                mixing_matrix(0, j)
            with pool.Fori(1, GROUPS) as g:
                for j in range(GROUP):
                    mixing_matrix(g, j)

        @block.tensor
        def _(pe):
            def transposes_x(g, j):
                t = tile_of(g, j)
                pe.wait_ge(ld_x[j], 16 * (g + 1))
                wait_past(pe, xT_h_ok, t)
                wait_past(pe, xT_l_ok, t)
                for k in range(DC):
                    last = pe.transpose(px[:, k * P:(k + 1) * P], x_sb[:, j, k * P:(k + 1) * P], ident[:])
                last.then_inc(xT_ps, 1)

            def product(g, j, half, ks):
                t = tile_of(g, j)
                if ks[0] == 0:
                    if half == 0:
                        pe.wait_ge(xT_h_ok, t + 1)
                        pe.wait_ge(xT_l_ok, t + 1)
                    wait_past(pe, u_h_ok[half], t)
                    wait_past(pe, u_l_ok[half], t)
                for k in ks:
                    if isinstance(g, int) and t == 0 and half == 0:
                        pe.wait_ge(wT_h_ok, k + 1)
                        pe.wait_ge(wT_l_ok, k + 1)
                    for n, (s, w) in enumerate(((xT_h, WT_h), (xT_h, WT_l), (xT_l, WT_h))):
                        last = pe.matmul(pu[half][:, 0:HC], s[:, j % 2, k, :], w[:, k, half, :],
                                         start=(k == 0 and n == 0), stop=(k == DC - 1 and n == 2))
                if ks[-1] == DC - 1:
                    last.then_inc(u_ps[half], 1)

            def mix(g, j):
                m = tile_of(g, j)
                par = j % 2
                pe.wait_ge(ablk_ok, m + 1)
                wait_past(pe, final_ok[par], nth_of_parity(g, j))
                for half in range(2):
                    pe.wait_ge(u_l_ok[half], m + 1)
                    for n, (s, w) in enumerate(((ablk_h, u_h), (ablk_h, u_l), (ablk_l, u_h))):
                        last = pe.matmul(pm[par][:, half, 0:HC], s[:, par].rearrange("p s o -> p (s o)"),
                                         w[:, j, half, :], start=(n == 0), stop=(n == 2))
                last.then_inc(mix_ps[par], 1)

            def z_transpose(g, j):
                m = tile_of(g, j)
                wait_past(pe, mT_l_ok, m)
                pe.wait_ge(z_ok, m + 1)
                pe.transpose(pzT, z[:].rearrange("p e r -> p (e r)"), ident[:]).then_inc(zT_ps, 1)

            def core_product(g, j):
                m = tile_of(g, j)
                pe.wait_ge(zT_h_ok, m + 1)
                pe.wait_ge(zT_l_ok, m + 1)
                for n, (s, w) in enumerate(((core_h, zT_h), (core_h, zT_l), (core_l, zT_h))):
                    last = pe.matmul(pmT, s[:], w[:], start=(n == 0), stop=(n == 2))
                last.then_inc(mT_ps, 1)

            def tail(g, j):
                m = tile_of(g, j)
                par = j % 2
                pe.wait_ge(mT_h_ok, m + 1)
                pe.wait_ge(mT_l_ok, m + 1)
                pe.wait_ge(brow_ok, m + 1)
                pe.wait_ge(small_ok, m + 1)
                for half in range(2):
                    last = pe.matmul(pm[par][:, half, 0:OH], tail_s[:, par, :],
                                     tail_w[:, half * OH:(half + 1) * OH],
                                     start=False, stop=True, skip_group_check=True)
                last.then_inc(tail_ps[par], 1)

            pe.wait_ge(ident_ok, 2)
            pe.wait_ge(ld_cond, 16)
            pe.transpose(pz[:, 0:P], cond_sb[:], ident[:]).then_inc(condT_ps, 1)
            pe.wait_ge(ld_ar, 32)
            for k in range(DC):
                last = pe.transpose(px[:, k * SM:(k + 1) * SM], ar_sb[:, k * P:(k + 1) * P], ident[0:SM, 0:SM])
            last.then_inc(arT_ps, 1)
            pe.wait_ge(ld_w0, 16)
            pe.wait_ge(condT_ok, 1)
            pe.matmul(pz[:, P:2 * P], W0_sb[:], condT[:], start=True, stop=True).then_inc(h1_ps, 1)
            pe.wait_ge(ld_wb, 32)

            def transposes_w(k):
                for c in range(O // P):
                    last = pe.transpose(pm[k // 2][:, k % 2, c * P:(c + 1) * P],
                                        Wb_sb[:, c, k * P:(k + 1) * P], ident[:])
                last.then_inc(wT_ps, 1)

            transposes_w(0)
            transposes_w(1)
            pe.wait_ge(ld_w1, 16)
            pe.wait_ge(h1_ok, 1)
            pe.matmul(pz[:, 0:P], W1_sb[:], h1T[:], start=True, stop=True).then_inc(h2_ps, 1)
            transposes_w(2)
            transposes_w(3)
            pe.wait_ge(arT_h_ok, 1)
            pe.wait_ge(arT_l_ok, 1)
            transposes_x(0, 0)
            pe.wait_ge(ld_w2, 16)
            pe.wait_ge(h2_ok, 1)
            pe.matmul(pz[:, P:P + KC], h2T[:], W2_sb[:], start=True, stop=True).then_inc(clog_ps, 1)

            def attention_transpose():
                pe.wait_ge(att_ok, 1)
                pe.transpose(pz[0:KC, 0:P], att[:], ident[:]).then_inc(attT_ps, 1)

            def aggregate():
                pe.wait_ge(ld_kw, 16)
                pe.wait_ge(ld_kb, 16)
                pe.wait_ge(attT_ok, 1)
                pe.wait_ge(wT_h_ok, DC)
                pe.wait_ge(wT_l_ok, DC)
                for h in range(2):
                    last = pe.matmul(pm[1][:, h, :],
                                     attT[:], kw[:, :, h * IH:(h + 1) * IH].rearrange("k o i -> k i o"),
                                     start=True, stop=True)
                last.then_inc(aggw_ps, 1)
                pe.matmul(pz[:, 0:CH], attT[:], kb[:, 0, :], start=True, stop=True)
                pe.matmul(pz[:, P:2 * P], kb[:].rearrange("k s o -> k (s o)"), attT[:],
                          start=True, stop=True).then_inc(aggb_ps, 1)

            def column_sums():
                pe.wait_ge(consts, 2)
                for half in range(2):
                    for k in range(DC):
                        for n, w in enumerate((WT_h, WT_l)):
                            last = pe.matmul(pm[0][:, half, 0:HC], ones_r[:], w[:, k, half, :],
                                             start=(k == 0 and n == 0), stop=(k == DC - 1 and n == 1))
                last.then_inc(wsum_ps, 1)

            def transposes_bw():
                pe.wait_ge(ld_bw, 16)
                pe.wait_ge(aggw_a, 1)
                pe.wait_ge(aggw_d, 1)
                for c in range(O // P):
                    last = pe.transpose(pm[1][0:R, 0, c * P:(c + 1) * P], Bw_sb[:, c, :], ident[:])
                last.then_inc(bwT_ps, 1)

            setup_at = {0: (attention_transpose,), 1: (aggregate,), 2: (column_sums, transposes_bw), 3: ()}
            for j in range(GROUP):
                transposes_x((j + 1) // GROUP, (j + 1) % GROUP)
                product(0, j, 0, range(DC))
                for stage in setup_at[j]:
                    stage()
                product(0, j, 1, range(DC))
            pe.wait_ge(core_l_ok, 1)
            pe.wait_ge(tail_rows, 16 * NBIAS)
            pe.wait_ge(bwT_h_ok, 2)
            pe.wait_ge(bwT_l_ok, 1)
            pe.wait_ge(aggb_col_ok, SPT)
            pe.wait_ge(wsum_s_ok, 1)

            def group(g, next_group):
                for j in range(GROUP):
                    mix(g - 1, j)
                    if j + 1 < GROUP:
                        transposes_x(g, j + 1)
                    elif next_group:
                        transposes_x(g + 1, 0)
                    product(g, j, 0, range(DC))
                    z_transpose(g - 1, j)
                    product(g, j, 1, range(DC // 2))
                    core_product(g - 1, j)
                    product(g, j, 1, range(DC // 2, DC))
                    tail(g - 1, j)

            group(1, True)
            with pe.Fori(2, GROUPS - 1) as g:
                group(g, True)
            group(GROUPS - 1, False)
            for j in range(GROUP):
                mix(GROUPS - 1, j)
                z_transpose(GROUPS - 1, j)
                core_product(GROUPS - 1, j)
                tail(GROUPS - 1, j)

        @block.scalar
        def _(act):
            act.dma_start(Wb_sb[:, 2:4, :],
                          W_base[2 * P:4 * P, :].rearrange("(c p) d -> p c d", p=P)).then_inc(ld_wb, 16)
            act.dma_start(ar_sb[0:R, :], A_w).then_inc(ld_ar, 16)
            act.dma_start(ar_sb[R:SM, :], router_w).then_inc(ld_ar, 16)
            act.dma_start(b0_col[:], b0.unsqueeze(1)).then_inc(ld_b01, 16)
            act.dma_start(b1_col[:], b1.unsqueeze(1)).then_inc(ld_b01, 16)

            def high_xT(g, j):
                act.wait_ge(xT_ps, tile_of(g, j) + 1)
                act.activation(xT_h[:, j % 2].rearrange("p c t -> p (c t)"), px[:], ACT.Copy).then_inc(xT_h_ok, 1)

            def high_u(g, j, half):
                act.wait_ge(u_ps[half], tile_of(g, j) + 1)
                act.activation(u_h[:, j, half, :], pu[half][:, 0:HC], ACT.Copy).then_inc(u_h_ok[half], 1)

            def exps(g, j):
                m = tile_of(g, j)
                act.wait_ge(nmax_ok, m + 1)
                act.activation(eprob[:], small[:, R:SM], ACT.Exp, bias=nmax[:, 0:1],
                               accum_out=esum[:, 0:1]).then_inc(eprob_ok, 1)

            def high_zT(g, j):
                act.wait_ge(zT_ps, tile_of(g, j) + 1)
                act.activation(zT_h[:], pzT, ACT.Copy).then_inc(zT_h_ok, 1)

            def high_mT(g, j):
                act.wait_ge(mT_ps, tile_of(g, j) + 1)
                act.activation(tail_s[0:BIAS, j % 2, :], pmT, ACT.Copy).then_inc(mT_h_ok, 1)

            def high_w(k):
                act.wait_ge(wT_ps, k + 1)
                act.activation(WT_h[:, k, :, 0:OH], pm[k // 2][:, k % 2, :].rearrange("p (h o) -> p h o", h=2),
                               ACT.Copy).then_inc(wT_h_ok, 1)

            act.wait_ge(arT_ps, 1)
            act.activation(WT_h[:, :, :, OH:HC],
                           px[:, 0:DC * SM].rearrange("p (c h s) -> p c h s", c=DC, h=2),
                           ACT.Copy).then_inc(arT_h_ok, 1)
            act.wait_ge(ld_b01, 32)
            act.wait_ge(h1_ps, 1)
            act.activation(h1T[:], pz[:, P:2 * P], ACT.Gelu, bias=b0_col[:, 0:1]).then_inc(h1_ok, 1)
            high_w(0)
            high_w(1)
            act.wait_ge(h2_ps, 1)
            act.activation(h2T[:], pz[:, 0:P], ACT.Gelu, bias=b1_col[:, 0:1]).then_inc(h2_ok, 1)
            high_w(2)
            high_w(3)
            high_xT(0, 0)
            high_xT(0, 1)
            act.wait_ge(cnmax_ok, 1)
            act.activation(cexp[:], clog[:], ACT.Exp, bias=cnmax[:, 0:1], accum_out=csum[:, 0:1]).then_inc(cexp_ok, 1)
            high_u(0, 0, 0)
            high_u(0, 0, 1)
            high_xT(0, 2)
            high_u(0, 1, 0)
            act.wait_ge(aggw_ps, 1)
            act.activation(aggw_sb[:, 0:IH, :].rearrange("b i o -> b (i o)"), pm[1][:, 0, :],
                           ACT.Copy).then_inc(aggw_a, 1)
            high_u(0, 1, 1)
            high_xT(0, 3)
            high_u(0, 2, 0)
            act.wait_ge(wsum_ps, 1)
            for r in range(0, 3, 2):
                act.activation(row_src[0:1, r, :].rearrange("p (h o) -> p h o", h=2), pm[0][0:1, :, 0:OH],
                               ACT.Copy).then_inc(row_h_ok, 1)
            act.wait_ge(ld_bb, 16)
            act.activation(row_src[0:1, 3, :], bb_row[:], ACT.Copy).then_inc(row_h_ok, 1)
            act.wait_ge(bwT_ps, 1)
            act.wait_ge(consts, 2)
            for row in (MID_H, MID_L):
                act.activation(tail_w[row:row + R, :], pm[1][0:R, 0, :], ACT.Copy, scale=SCALING).then_inc(bwT_h_ok, 1)
            high_u(0, 2, 1)
            act.wait_ge(ld_cores, 16)
            act.wait_ge(consts, 2)
            act.activation(core_h[:].rearrange("p (n c) -> p n c", n=3)[:, :, 0:R],
                           cores_sb[:].unsqueeze(1).to_broadcast([P, 3, R]), ACT.Copy).then_inc(core_h_ok, 1)
            high_xT(1, 0)
            high_u(0, 3, 0)
            high_u(0, 3, 1)

            def group(g, next_group):
                for j in range(GROUP):
                    exps(g - 1, j)
                    if j + 1 < GROUP:
                        high_xT(g, j + 1)
                    elif next_group:
                        high_xT(g + 1, 0)
                    high_zT(g - 1, j)
                    high_u(g, j, 0)
                    high_mT(g - 1, j)
                    high_u(g, j, 1)

            group(1, True)
            with act.Fori(2, GROUPS - 1) as g:
                group(g, True)
            group(GROUPS - 1, False)
            for j in range(GROUP):
                exps(GROUPS - 1, j)
                high_zT(GROUPS - 1, j)
                high_mT(GROUPS - 1, j)

        @block.vector
        def _(dve):
            def low(out_, psum, high):
                return dve.tensor_tensor(out_, psum, high.bitcast(F32), ALU.subtract)

            def low_xT(g, j):
                dve.wait_ge(xT_h_ok, tile_of(g, j) + 1)
                low(xT_l[:, j % 2].rearrange("p c t -> p (c t)"), px[:],
                    xT_h[:, j % 2].rearrange("p c t -> p (c t)")).then_inc(xT_l_ok, 1)

            def low_u(g, j, half):
                dve.wait_ge(u_h_ok[half], tile_of(g, j) + 1)
                low(u_l[:, j, half, :], pu[half][:, 0:HC], u_h[:, j, half, :]).then_inc(u_l_ok[half], 1)

            def small_columns(g, j):
                m = tile_of(g, j)
                par = j % 2
                dve.wait_ge(mix_ps[par], nth_of_parity(g, j) + 1)
                wait_past(dve, z_ok, m)
                dve.scalar_tensor_tensor(out=small[:].rearrange("p (h s) -> p h s", h=2),
                                         in0=wsum_s[:].rearrange("p (h s) -> p h s", h=2),
                                         scalar=aggb_col[:, bass.ds(m, 1)],
                                         in1=pm[par][:, :, OH:HC],
                                         op0=ALU.mult, op1=ALU.add).then_inc(small_ok, 1)
                dve.wait_ge(small_ok, m + 1)
                dve.tensor_reduce(nmax[:], small[:, R:SM], AX_X, ALU.max, negate=True).then_inc(nmax_ok, 1)

            def routed(g, j):
                m = tile_of(g, j)
                dve.wait_ge(eprob_ok, m + 1)
                dve.reciprocal(rinv[:], esum[:]).then_inc(rinv_ok, 1)
                dve.wait_ge(rinv_ok, m + 1)
                wait_past(dve, zT_ps, m)
                dve.scalar_tensor_tensor(out=z[:], in0=small[:, 0:R].unsqueeze(1).to_broadcast([P, E, R]),
                                         scalar=rinv[:, 0:1], in1=eprob[:].unsqueeze(2).to_broadcast([P, E, R]),
                                         op0=ALU.mult, op1=ALU.mult).then_inc(z_ok, 1)

            def low_zT(g, j):
                dve.wait_ge(zT_h_ok, tile_of(g, j) + 1)
                low(zT_l[:], pzT, zT_h[:]).then_inc(zT_l_ok, 1)

            def low_mT(g, j):
                dve.wait_ge(mT_h_ok, tile_of(g, j) + 1)
                low(tail_s[MID_L:MID_L + R, j % 2, :], pz[MID_L:MID_L + R, P:2 * P],
                    tail_s[MID_L:MID_L + R, j % 2, :]).then_inc(mT_l_ok, 1)

            def final(g, j):
                par = j % 2
                dve.wait_ge(tail_ps[par], nth_of_parity(g, j) + 1)
                dve.wait_ge(x_kept[j], 16 * (g + 1))
                wait_past(dve, stored[j], 16 * g)
                dve.tensor_tensor(out_sb[:, j, :].rearrange("p (h o) -> p h o", h=2), pm[par][:, :, 0:OH],
                                  xres[:, j, :].rearrange("p (h o) -> p h o", h=2),
                                  ALU.add).then_inc(final_ok[par], 1)

            def low_w(k):
                dve.wait_ge(wT_h_ok, k + 1)
                low(WT_l[:, k, :, 0:OH], pm[k // 2][:, k % 2, :].rearrange("p (h o) -> p h o", h=2),
                    WT_h[:, k, :, 0:OH]).then_inc(wT_l_ok, 1)

            dve.memset(samemask[:], 0.0).then_inc(consts, 1)
            dve.memset(core_h[:].bitcast(F32), 0.0)
            dve.memset(core_l[:].bitcast(F32), 0.0)
            dve.memset(tail_w[:].bitcast(F32), 0.0)
            dve.memset(ones_r[:].bitcast(F32), 1.0).then_inc(consts, 1)
            dve.wait_ge(consts, 2)
            for s in range(SPT):
                dve.memset(samemask[s * CH:(s + 1) * CH, s:s + 1], 1.0).then_inc(consts, 1)
            dve.wait_ge(condT_ps, 1)
            dve.tensor_copy(condT[:], pz[:, 0:P]).then_inc(condT_ok, 1)
            dve.wait_ge(arT_h_ok, 1)
            low(WT_l[:, :, :, OH:HC], px[:, 0:DC * SM].rearrange("p (c h s) -> p c h s", c=DC, h=2),
                WT_h[:, :, :, OH:HC]).then_inc(arT_l_ok, 1)
            for k in range(DC):
                low_w(k)
            low_xT(0, 0)
            dve.wait_ge(ld_b2, 16)
            dve.wait_ge(clog_ps, 1)
            dve.tensor_tensor(clog[:], pz[:, P:P + KC], b2_bc[:], ALU.add).then_inc(clog_ok, 1)
            dve.wait_ge(clog_ok, 1)
            dve.tensor_reduce(cnmax[:], clog[:], AX_X, ALU.max, negate=True).then_inc(cnmax_ok, 1)
            low_xT(0, 1)
            dve.wait_ge(cexp_ok, 1)
            dve.reciprocal(crinv[:], csum[:]).then_inc(crinv_ok, 1)
            dve.wait_ge(crinv_ok, 1)
            dve.tensor_scalar(att[:], cexp[:], crinv[:, 0:1], None, ALU.mult).then_inc(att_ok, 1)
            low_u(0, 0, 0)
            dve.wait_ge(attT_ps, 1)
            dve.tensor_copy(attT[:], pz[0:KC, 0:P]).then_inc(attT_ok, 1)
            low_u(0, 0, 1)
            low_xT(0, 2)
            low_u(0, 1, 0)
            dve.wait_ge(aggw_ps, 1)
            dve.tensor_copy(aggw_sb[:, IH:CH, :].rearrange("b i o -> b (i o)"), pm[1][:, 1, :]).then_inc(aggw_d, 1)
            dve.wait_ge(aggb_ps, 1)
            dve.tensor_copy(aggb_hl[:, 0, :], pz[:, 0:CH]).then_inc(aggb_hl_ok, 1)
            dve.wait_ge(aggb_hl_ok, 1)
            low(aggb_hl[:, 1, :], pz[:, 0:CH], aggb_hl[:, 0, :]).then_inc(aggb_hl_ok, 1)
            low_u(0, 1, 1)
            low_xT(0, 3)
            for s in range(SPT):
                dve.tensor_copy(aggb_col[s * CH:(s + 1) * CH, :],
                                pz[s * CH:(s + 1) * CH, P:2 * P].rearrange("p (t s) -> p s t", s=SPT)[:, s, :]
                                ).then_inc(aggb_col_ok, 1)
            low_u(0, 2, 0)
            dve.wait_ge(row_h_ok, 2)
            low(row_src[0:1, 1, :].rearrange("p (h o) -> p h o", h=2), pm[0][0:1, :, 0:OH],
                row_src[0:1, 0, :].rearrange("p (h o) -> p h o", h=2)).then_inc(row_l_ok, 1)
            dve.tensor_copy(wsum_s[:].rearrange("p (h s) -> p h s", h=2), pm[0][:, :, OH:HC]).then_inc(wsum_s_ok, 1)
            dve.wait_ge(row_h_ok, 3)
            low(row_src[0:1, 4, :], bb_row[:], row_src[0:1, 3, :]).then_inc(row_l_ok, 1)
            dve.wait_ge(bwT_h_ok, 2)
            dve.scalar_tensor_tensor(out=tail_w[MID_H2:MID_H2 + R, :], in0=pm[1][0:R, 0, :], scalar=SCALING,
                                     in1=tail_w[MID_H:MID_H + R, :].bitcast(F32),
                                     op0=ALU.mult, op1=ALU.subtract).then_inc(bwT_l_ok, 1)
            low_u(0, 2, 1)
            dve.wait_ge(core_h_ok, 1)
            low(core_l[:, 0:R], cores_sb[:], core_h[:, 0:R])
            for row in (MID_L, MID_H2):
                last = low(core_l[:, row:row + R], cores_sb[:], core_h[:, 0:R])
            last.then_inc(core_l_ok, 1)
            low_xT(1, 0)
            low_u(0, 3, 0)
            dve.wait_ge(wsum_s_ok, 1)
            dve.wait_ge(aggb_col_ok, SPT)

            def group(g, next_group):
                for j in range(GROUP):
                    small_columns(g - 1, j)
                    if j == 0:
                        low_u(g - 1, GROUP - 1, 1)
                    else:
                        low_u(g, j - 1, 1)
                    routed(g - 1, j)
                    if j + 1 < GROUP:
                        low_xT(g, j + 1)
                    elif next_group:
                        low_xT(g + 1, 0)
                    low_zT(g - 1, j)
                    low_u(g, j, 0)
                    low_mT(g - 1, j)
                    final(g - 1, j)

            group(1, True)
            with dve.Fori(2, GROUPS - 1) as g:
                group(g, True)
            group(GROUPS - 1, False)
            for j in range(GROUP):
                small_columns(GROUPS - 1, j)
                if j == 0:
                    low_u(GROUPS - 1, GROUP - 1, 1)
                routed(GROUPS - 1, j)
                low_zT(GROUPS - 1, j)
                low_mT(GROUPS - 1, j)
                final(GROUPS - 1, j)


_INS = ['x', 'cond_128', 'L0_cond_W0', 'L0_cond_b0', 'L0_cond_W1', 'L0_cond_b1', 'L0_cond_W2', 'L0_cond_b2',
        'L0_cond_weight', 'L0_cond_bias_k', 'L0_ffn_W_base', 'L0_ffn_b_base', 'L0_ffn_A_w', 'L0_ffn_B_w',
        'L0_ffn_router_w', 'L0_ffn_cores']


def kernel(**inputs):
    import numpy as _np
    import concourse.bacc as _bacc
    from concourse import mybir as _mybir
    from concourse.bass_utils import run_bass_kernel_spmd as _run

    nc = _bacc.Bacc("TRN2", target_bir_lowering=False, num_devices=1)
    arrays, args = {}, []
    for name in _INS:
        a = _np.ascontiguousarray(inputs[name])
        arrays[f"in_{name}_dram"] = a
        args.append(nc.dram_tensor(f"in_{name}_dram", a.shape, _mybir.dt.from_np(a.dtype), kind="ExternalInput").ap())
    out = nc.dram_tensor("out_0_dram", inputs['x'].shape, _mybir.dt.float32, kind="ExternalOutput").ap()
    adaln_ffn(nc, *args, out)
    r = _run(nc, [arrays], core_ids=[0])
    return r.results[0]["out_0_dram"]
```

```python
from contextlib import ExitStack

import concourse.bass as bass
from concourse import mybir

F32 = mybir.dt.float32
F32R = mybir.dt.float32r
ALU = mybir.AluOpType
ACT = mybir.ActivationFunctionType
AX_X = mybir.AxisListType.X

P = 128
GROUP = 4
LAG = 2
WARM = (9, 5, 4, 0)


def adaln_ffn(nc, x, cond, W0, b0, W1, b1, W2, b2, weight, bias_k, W_base, b_base, A_w, B_w,
              router_w, cores, out):
    BATCH, CH, D = x.shape
    KC = W2.shape[1]
    O = W_base.shape[0]
    E, R, _ = cores.shape
    SPT = P // CH
    TILES = BATCH * CH // P
    GROUPS = TILES // GROUP
    DC = D // P
    OH = O // 2
    SM = R + E
    SH = SM // 2
    HC = OH + SH
    SCALING = 2.0
    IH = CH // 2
    assert E * R == P and O % 2 == 0 and D % P == 0 and TILES % GROUP == 0
    MID_H, MID_L, MID_H2, BIAS = 0, 32, 64, 96
    NBIAS = 5

    x_t = x.rearrange("(g j s) c d -> g j (s c) d", j=GROUP, s=SPT)
    out_t = out.rearrange("(g j s) c d -> g j (s c) d", j=GROUP, s=SPT)

    with ExitStack() as ctx:
        def sb(name, shape, dt=F32):
            return ctx.enter_context(nc.sbuf_tensor(name, shape, dt))

        def ps(name, shape):
            return ctx.enter_context(nc.psum_tensor(name, shape, F32))

        def sem(name):
            return ctx.enter_context(nc.semaphore(name))

        ident = sb("ident", [P, P])
        ones_r = sb("ones_r", [P, P], F32R)
        gelu_one = sb("gelu_one", [P, 1])
        samemask = sb("samemask", [P, SPT])
        cond_sb = sb("cond_sb", [P, P])
        condT = sb("condT", [P, P])
        W0_sb = sb("W0_sb", [P, P])
        W1_sb = sb("W1_sb", [P, P])
        W2_sb = sb("W2_sb", [P, KC])
        b0_col = sb("b0_col", [P, 1])
        b1_col = sb("b1_col", [P, 1])
        b2_bc = sb("b2_bc", [P, KC])
        h1T = sb("h1T", [P, P])
        h2T = sb("h2T", [P, P])
        clog = sb("clog", [P, KC])
        cnmax = sb("cnmax", [P, 1])
        cexp = sb("cexp", [P, KC])
        csum = sb("csum", [P, 1])
        crinv = sb("crinv", [P, 1])
        att = sb("att", [P, KC])
        attT = sb("attT", [KC, P])
        kw = sb("kw", [KC, CH, CH])
        kb = sb("kb", [KC, SPT, CH])
        aggw_sb = sb("aggw_sb", [P, CH, CH])
        aggb_hl = sb("aggb_hl", [P, 2, CH], F32R)
        aggw_c = sb("aggw_c", [P, TILES, CH])
        aggb_col = sb("aggb_col", [P, TILES])
        bias_rows = sb("bias_rows", [P, TILES * P])
        Wb_sb = sb("Wb_sb", [P, O // P, D])
        ar_sb = sb("ar_sb", [SM, D])
        Bw_sb = sb("Bw_sb", [P, O // P, R])
        bb_row = sb("bb_row", [1, O])
        cores_sb = sb("cores_sb", [P, R])
        WT_h = sb("WT_h", [P, DC, 2, HC], F32R)
        WT_l = sb("WT_l", [P, DC, 2, HC], F32R)
        wsum_s = sb("wsum_s", [P, SM])
        row_src = sb("row_src", [1, NBIAS, O], F32R)
        core_h = sb("core_h", [P, BIAS], F32R)
        core_l = sb("core_l", [P, BIAS], F32R)
        tail_w = sb("tail_w", [P, O], F32R)
        x_sb = sb("x_sb", [P, GROUP, D])
        xres = sb("xres", [P, GROUP, D])
        xT_h = sb("xT_h", [P, 2, DC, P], F32R)
        xT_l = sb("xT_l", [P, 2, DC, P], F32R)
        u_h = sb("u_h", [P, GROUP, 2, HC], F32R)
        u_l = sb("u_l", [P, GROUP, 2, HC], F32R)
        ablk = sb("ablk", [P, SPT, CH])
        ablk_h = sb("ablk_h", [P, 2, SPT, CH], F32R)
        ablk_l = sb("ablk_l", [P, 2, SPT, CH], F32R)
        small = sb("small", [P, SM])
        nmax = sb("nmax", [P, 1])
        eprob = sb("eprob", [P, E])
        esum = sb("esum", [P, 1])
        rinv = sb("rinv", [P, 1])
        z = sb("z", [P, E, R])
        zT_h = sb("zT_h", [P, P], F32R)
        zT_l = sb("zT_l", [P, P], F32R)
        tail_s = sb("tail_s", [P, 2, P], F32R)
        out_sb = sb("out_sb", [P, GROUP, O])

        pm = [ps("pm0", [P, 2, 512]), ps("pm1", [P, 2, 512])]
        pu = [ps("pu0", [P, 512]), ps("pu1", [P, 512])]
        px = ps("px", [P, 512])
        pz = ps("pz", [P, 512])
        pzT = pz[:, 0:P]
        pmT = pz[0:BIAS, P:2 * P]

        aggw_dram = nc.dram_tensor("aggw_scratch", (TILES, P, CH), F32).ap()

        ld_cond, ld_w0, ld_w1, ld_w2 = sem("ld_cond"), sem("ld_w0"), sem("ld_w1"), sem("ld_w2")
        ld_b01, ld_b2, ld_kw, ld_kb = sem("ld_b01"), sem("ld_b2"), sem("ld_kw"), sem("ld_kb")
        ld_ar, ld_bw, ld_bb = sem("ld_ar"), sem("ld_bw"), sem("ld_bb")
        ld_wb = [sem(f"ld_wb{k}") for k in range(DC)]
        ld_cores = sem("ld_cores")
        ld_x = [sem(f"ld_x{j}") for j in range(GROUP)]
        x_kept = [sem(f"x_kept{j}") for j in range(GROUP)]
        stored = [sem(f"stored{j}") for j in range(GROUP)]
        scratch_out, aggw_back, rows_back = sem("scratch_out"), sem("aggw_back"), sem("rows_back")
        tail_rows = sem("tail_rows")
        consts, ident_ok, rows_set = sem("consts"), sem("ident_ok"), sem("rows_set")
        condT_ps, condT_ok = sem("condT_ps"), sem("condT_ok")
        h1_ps, h1_ok, h2_ps, h2_ok = sem("h1_ps"), sem("h1_ok"), sem("h2_ps"), sem("h2_ok")
        clog_ps, clog_ok, cnmax_ok, cexp_ok = sem("clog_ps"), sem("clog_ok"), sem("cnmax_ok"), sem("cexp_ok")
        crinv_ok, att_ok, attT_ps, attT_ok = sem("crinv_ok"), sem("att_ok"), sem("attT_ps"), sem("attT_ok")
        aggw_ps, aggw_a, aggw_d = sem("aggw_ps"), sem("aggw_a"), sem("aggw_d")
        aggb_ps, aggb_hl_ok, aggb_col_ok = sem("aggb_ps"), sem("aggb_hl_ok"), sem("aggb_col_ok")
        arT_ps, arT_h_ok, arT_l_ok = sem("arT_ps"), sem("arT_h_ok"), sem("arT_l_ok")
        wT_ps, wT_h_ok, wT_l_ok = sem("wT_ps"), sem("wT_h_ok"), sem("wT_l_ok")
        wsum_ps, row_h_ok, row_l_ok, wsum_s_ok = sem("wsum_ps"), sem("row_h_ok"), sem("row_l_ok"), sem("wsum_s_ok")
        bwT_ps, bwT_h_ok, bwT_l_ok = sem("bwT_ps"), sem("bwT_h_ok"), sem("bwT_l_ok")
        core_h_ok, core_l_ok = sem("core_h_ok"), sem("core_l_ok")
        xT_ps, xT_h_ok, xT_l_ok = sem("xT_ps"), sem("xT_h_ok"), sem("xT_l_ok")
        u_ps = [sem("u_ps0"), sem("u_ps1")]
        u_h_ok = [sem("u_h_ok0"), sem("u_h_ok1")]
        u_l_ok = [sem("u_l_ok0"), sem("u_l_ok1")]
        small_ok, nmax_ok, eprob_ok, rinv_ok, z_ok = (
            sem("small_ok"), sem("nmax_ok"), sem("eprob_ok"), sem("rinv_ok"), sem("z_ok"))
        zT_ps, zT_h_ok, zT_l_ok = sem("zT_ps"), sem("zT_h_ok"), sem("zT_l_ok")
        mT_ps, mT_h_ok, mT_l_ok = sem("mT_ps"), sem("mT_h_ok"), sem("mT_l_ok")
        ablk_f_ok, ablk_h_ok, ablk_ok, brow_ok = (
            sem("ablk_f_ok"), sem("ablk_h_ok"), sem("ablk_ok"), sem("brow_ok"))
        mix_ps = [sem("mix_ps0"), sem("mix_ps1")]
        tail_ps = [sem("tail_ps0"), sem("tail_ps1")]
        final_ok = [sem("final_ok0"), sem("final_ok1")]

        block = ctx.enter_context(nc.Block())

        def tile_of(g, j):
            return g * GROUP + j

        def nth_of_parity(g, j):
            return g * (GROUP // 2) + j // 2

        def wait_past(eng, semaphore, n):
            if not (isinstance(n, int) and n <= 0):
                eng.wait_ge(semaphore, n)

        def back(g, j, n):
            return (g, j - n) if j >= n else (g - 1, j - n + GROUP)

        def ahead(g, j):
            return (g, j + 1) if j + 1 < GROUP else (g + 1, 0)

        def real(g, j):
            return not isinstance(g, int) or 0 <= tile_of(g, j) < TILES

        def first(g, j, t):
            return isinstance(g, int) and tile_of(g, j) == t

        def run(eng, step, before_loop=None):
            for j in range(GROUP):
                step(0, j)
                if before_loop:
                    before_loop(j)
            for j in range(GROUP):
                step(1, j)
            with eng.Fori(2, GROUPS - 1) as g:
                for j in range(GROUP):
                    step(g, j)
            for j in range(GROUP):
                step(GROUPS - 1, j)
            for j in range(LAG + 1):
                step(GROUPS, j)

        @block.sync
        def _(sp):
            def load_wb(k):
                sp.dma_start(Wb_sb[:, :, k * P:(k + 1) * P],
                             W_base[:, k * P:(k + 1) * P].rearrange("(c p) d -> p c d", p=P)).then_inc(ld_wb[k], 16)

            sp.dma_start(cond_sb[:], cond).then_inc(ld_cond, 16)
            sp.dma_start(W0_sb[:], W0).then_inc(ld_w0, 16)
            sp.dma_start(W1_sb[:], W1).then_inc(ld_w1, 16)
            sp.dma_start(x_sb[:, 0, :], x_t[0, 0]).then_inc(ld_x[0], 16)
            load_wb(0)
            load_wb(1)
            sp.dma_start(ar_sb[0:R, :], A_w).then_inc(ld_ar, 16)
            sp.dma_start(ar_sb[R:SM, :], router_w).then_inc(ld_ar, 16)
            load_wb(2)
            load_wb(3)
            for j in range(1, GROUP):
                sp.dma_start(x_sb[:, j, :], x_t[0, j]).then_inc(ld_x[j], 16)
            sp.dma_start(Bw_sb[:], B_w.rearrange("(c p) r -> p c r", p=P)).then_inc(ld_bw, 16)
            sp.dma_start(bb_row[:], b_base.unsqueeze(0)).then_inc(ld_bb, 16)

            sp.wait_ge(aggw_a, 1)
            sp.wait_ge(aggw_d, 1)
            sp.dma_start(aggw_dram.rearrange("t (s i) o -> (t s) (i o)", s=SPT),
                         aggw_sb[:].rearrange("b i o -> b (i o)")).then_inc(scratch_out, 16)
            sp.wait_ge(scratch_out, 16)
            sp.dma_start(aggw_c[:], aggw_dram.rearrange("t p o -> p t o")).then_inc(aggw_back, 16)
            sp.wait_ge(rows_set, 1)
            sp.wait_ge(aggb_hl_ok, 2)
            for r, part in enumerate((0, 0, 1)):
                sp.dma_start(bias_rows[BIAS + r:BIAS + r + 1, :],
                             aggb_hl[:, part, :].bitcast(F32)).then_inc(rows_back, 16)

            def store(g, j):
                sp.wait_ge(final_ok[j % 2], nth_of_parity(g, j) + 1)
                sp.dma_start(out_t[g, j], out_sb[:, j, :]).then_inc(stored[j], 16)

            def keep_x(g, j):
                sp.wait_ge(ld_x[j], 16 * (g + 1))
                sp.dma_start(xres[:, j, :], x_sb[:, j, :]).then_inc(x_kept[j], 16)

            def next_x(g, j):
                sp.wait_ge(xT_ps, tile_of(g, j) + 1)
                sp.wait_ge(x_kept[j], 16 * (g + 1))
                sp.dma_start(x_sb[:, j, :], x_t[g + 1, j]).then_inc(ld_x[j], 16)

            def step(g, j):
                r = back(g, j, LAG + 1)
                if real(*r):
                    store(*r)
                if real(g, j):
                    keep_x(g, j)
                    if real(g + 1, j):
                        next_x(g, j)

            def bias_rows_of_tail(j):
                if j == 0:
                    sp.wait_ge(row_h_ok, 3)
                    sp.wait_ge(row_l_ok, 2)
                    for r in range(NBIAS):
                        sp.dma_start(tail_w[BIAS + r:BIAS + r + 1, :].bitcast(F32),
                                     row_src[0:1, r, :].bitcast(F32)).then_inc(tail_rows, 16)

            run(sp, step, bias_rows_of_tail)
            for j in range(GROUP):
                sp.wait_ge(stored[j], 16 * GROUPS)

        @block.gpsimd
        def _(pool):
            pool.memset(ident[:], 0.0).then_inc(ident_ok, 1)
            pool.wait_ge(ident_ok, 1)
            pool.affine_select(out=ident[:], in_=ident[:], compare_op=ALU.not_equal, fill=1.0, base=0,
                               pattern=[[-1, P]], channel_multiplier=1).then_inc(ident_ok, 1)
            pool.dma_start(b0_col[:], b0.unsqueeze(1)).then_inc(ld_b01, 16)
            pool.dma_start(b1_col[:], b1.unsqueeze(1)).then_inc(ld_b01, 16)
            pool.dma_start(W2_sb[:], W2).then_inc(ld_w2, 16)
            pool.dma_start(b2_bc[:], b2.unsqueeze(0).to_broadcast([P, KC])).then_inc(ld_b2, 16)
            pool.dma_start(kw[:], weight.rearrange("k o i one -> k o (i one)")).then_inc(ld_kw, 16)
            pool.dma_start(kb[:], bias_k.unsqueeze(1).to_broadcast([KC, SPT, CH])).then_inc(ld_kb, 16)
            pool.dma_start(cores_sb[:], cores.rearrange("e r q -> (e r) q")).then_inc(ld_cores, 16)
            pool.wait_ge(ident_ok, 2)
            pool.memset(bias_rows[BIAS:P, :], 1.0).then_inc(rows_set, 1)
            pool.wait_ge(rows_set, 1)
            pool.wait_ge(consts, 2 + SPT)
            pool.wait_ge(aggw_back, 16)

            def mixing_matrix(g, j):
                m = tile_of(g, j)
                par = j % 2
                wait_past(pool, ablk_ok, m)
                wait_past(pool, brow_ok, m)
                wait_past(pool, mix_ps[par], nth_of_parity(g, j))
                aggw_t = aggw_c[:, bass.ds(m, 1), :].to_broadcast([P, SPT, CH])
                mask = samemask[:].unsqueeze(2).to_broadcast([P, SPT, CH])
                pool.tensor_tensor(ablk[:], aggw_t, mask, ALU.mult).then_inc(ablk_f_ok, 1)
                pool.tensor_tensor(ablk_h[:, par], aggw_t, mask, ALU.mult).then_inc(ablk_h_ok, 1)
                pool.wait_ge(ablk_f_ok, m + 1)
                pool.wait_ge(ablk_h_ok, m + 1)
                pool.tensor_tensor(ablk_l[:, par], ablk[:], ablk_h[:, par].bitcast(F32),
                                   ALU.subtract).then_inc(ablk_ok, 1)
                if first(g, j, 0):
                    pool.wait_ge(rows_back, 16 * 3)
                wait_past(pool, tail_ps[par], nth_of_parity(g, j))
                pool.wait_ge(ablk_ok, m + 1)
                pool.tensor_copy(tail_s[BIAS:P, par, :],
                                 bias_rows[BIAS:P, bass.ds(m * P, P)]).then_inc(brow_ok, 1)

            for j in range(GROUP):
                mixing_matrix(0, j)
            with pool.Fori(1, GROUPS) as g:
                for j in range(GROUP):
                    mixing_matrix(g, j)

        @block.tensor
        def _(pe):
            def transposes_x(g, j):
                t = tile_of(g, j)
                pe.wait_ge(ld_x[j], 16 * (g + 1))
                wait_past(pe, xT_l_ok, t)
                for k in range(DC):
                    last = pe.transpose(px[:, k * P:(k + 1) * P], x_sb[:, j, k * P:(k + 1) * P], ident[:])
                last.then_inc(xT_ps, 1)

            def product(g, j, half):
                t = tile_of(g, j)
                if half == 0:
                    pe.wait_ge(xT_l_ok, t + 1)
                wait_past(pe, u_l_ok[half], t)
                for k in range(DC):
                    if first(g, j, 0) and half == 0:
                        pe.wait_ge(wT_l_ok, k + 1)
                    for n, (s, w) in enumerate(((xT_h, WT_h), (xT_h, WT_l), (xT_l, WT_h))):
                        last = pe.matmul(pu[half][:, 0:HC], s[:, j % 2, k, :], w[:, k, half, :],
                                         start=(k == 0 and n == 0), stop=(k == DC - 1 and n == 2))
                last.then_inc(u_ps[half], 1)

            def mix(g, j):
                m = tile_of(g, j)
                par = j % 2
                pe.wait_ge(ablk_ok, m + 1)
                wait_past(pe, final_ok[par], nth_of_parity(g, j))
                for half in range(2):
                    pe.wait_ge(u_l_ok[half], m + 1)
                    for n, (s, w) in enumerate(((ablk_h, u_h), (ablk_h, u_l), (ablk_l, u_h))):
                        last = pe.matmul(pm[par][:, half, 0:HC], s[:, par].rearrange("p s o -> p (s o)"),
                                         w[:, j, half, :], start=(n == 0), stop=(n == 2))
                last.then_inc(mix_ps[par], 1)

            def z_transpose(g, j):
                m = tile_of(g, j)
                wait_past(pe, mT_l_ok, m)
                pe.wait_ge(z_ok, m + 1)
                pe.transpose(pzT, z[:].rearrange("p e r -> p (e r)"), ident[:]).then_inc(zT_ps, 1)

            def core_product(g, j):
                pe.wait_ge(zT_l_ok, tile_of(g, j) + 1)
                for n, (s, w) in enumerate(((core_h, zT_h), (core_h, zT_l), (core_l, zT_h))):
                    last = pe.matmul(pmT, s[:], w[:], start=(n == 0), stop=(n == 2))
                last.then_inc(mT_ps, 1)

            def tail(g, j):
                m = tile_of(g, j)
                par = j % 2
                pe.wait_ge(mT_l_ok, m + 1)
                pe.wait_ge(brow_ok, m + 1)
                for half in range(2):
                    last = pe.matmul(pm[par][:, half, 0:OH], tail_s[:, par, :],
                                     tail_w[:, half * OH:(half + 1) * OH],
                                     start=False, stop=True, skip_group_check=True)
                last.then_inc(tail_ps[par], 1)

            def keep_busy(n):
                for _ in range(n):
                    pe.transpose(pm[1][:, 1, 0:P], ident[:], ident[:])

            def transposes_w(k):
                pe.wait_ge(ld_wb[k], 16)
                for c in range(O // P):
                    last = pe.transpose(pm[k // 2][:, k % 2, c * P:(c + 1) * P],
                                        Wb_sb[:, c, k * P:(k + 1) * P], ident[:])
                last.then_inc(wT_ps, 1)

            pe.wait_ge(ident_ok, 2)
            keep_busy(WARM[0])
            pe.wait_ge(ld_cond, 16)
            pe.transpose(pz[:, 0:P], cond_sb[:], ident[:]).then_inc(condT_ps, 1)
            keep_busy(WARM[1])
            pe.wait_ge(ld_w0, 16)
            pe.wait_ge(condT_ok, 1)
            pe.matmul(pz[:, P:2 * P], W0_sb[:], condT[:], start=True, stop=True).then_inc(h1_ps, 1)
            keep_busy(WARM[2])
            pe.wait_ge(ld_w1, 16)
            pe.wait_ge(h1_ok, 1)
            pe.matmul(pz[:, 0:P], W1_sb[:], h1T[:], start=True, stop=True).then_inc(h2_ps, 1)
            transposes_x(0, 0)
            keep_busy(WARM[3])
            pe.wait_ge(ld_w2, 16)
            pe.wait_ge(h2_ok, 1)
            pe.matmul(pz[:, P:P + KC], h2T[:], W2_sb[:], start=True, stop=True).then_inc(clog_ps, 1)
            transposes_w(0)
            transposes_w(1)
            pe.wait_ge(ld_ar, 32)
            for k in range(DC):
                last = pe.transpose(pu[1][:, k * SM:(k + 1) * SM], ar_sb[:, k * P:(k + 1) * P], ident[0:SM, 0:SM])
            last.then_inc(arT_ps, 1)
            pe.wait_ge(att_ok, 1)
            pe.transpose(pz[0:KC, 0:P], att[:], ident[:]).then_inc(attT_ps, 1)
            transposes_w(2)
            pe.wait_ge(ld_kw, 16)
            pe.wait_ge(ld_kb, 16)
            pe.wait_ge(attT_ok, 1)
            pe.wait_ge(arT_l_ok, 1)
            for h in range(2):
                pe.matmul(pu[h][:], attT[:], kw[:, :, h * IH:(h + 1) * IH].rearrange("k o i -> k i o"),
                          start=True, stop=True).then_inc(aggw_ps, 1)
            pe.matmul(pz[:, 0:CH], attT[:], kb[:, 0, :], start=True, stop=True)
            pe.matmul(pz[:, P:2 * P], kb[:].rearrange("k s o -> k (s o)"), attT[:],
                      start=True, stop=True).then_inc(aggb_ps, 1)
            transposes_w(3)

            def column_sums():
                pe.wait_ge(consts, 2)
                pe.wait_ge(wT_l_ok, DC)
                for half in range(2):
                    for k in range(DC):
                        for n, w in enumerate((WT_h, WT_l)):
                            last = pe.matmul(pm[0][:, half, 0:HC], ones_r[:], w[:, k, half, :],
                                             start=(k == 0 and n == 0), stop=(k == DC - 1 and n == 1))
                last.then_inc(wsum_ps, 1)

            def transposes_bw():
                pe.wait_ge(ld_bw, 16)
                for c in range(O // P):
                    last = pe.transpose(pm[1][0:R, 0, c * P:(c + 1) * P], Bw_sb[:, c, :], ident[:])
                last.then_inc(bwT_ps, 1)

            def step(g, j):
                m, r = back(g, j, LAG), back(g, j, LAG + 1)
                if first(g, j, 0):
                    pe.wait_ge(aggw_a, 1)
                    pe.wait_ge(aggw_d, 1)
                if first(g, j, LAG):
                    pe.wait_ge(wsum_s_ok, 1)
                    pe.wait_ge(row_l_ok, 1)
                if first(g, j, LAG + 1):
                    pe.wait_ge(bwT_l_ok, 1)
                    pe.wait_ge(tail_rows, 16 * NBIAS)
                if real(*m):
                    mix(*m)
                if real(*ahead(g, j)):
                    transposes_x(*ahead(g, j))
                if real(*r):
                    tail(*r)
                if real(g, j):
                    product(g, j, 0)
                if first(g, j, 0):
                    column_sums()
                    transposes_bw()
                if first(g, j, LAG):
                    pe.wait_ge(aggb_col_ok, SPT)
                    pe.wait_ge(core_l_ok, 1)
                if real(*m):
                    z_transpose(*m)
                if real(g, j):
                    product(g, j, 1)
                if real(*m):
                    core_product(*m)

            run(pe, step)

        @block.scalar
        def _(act):
            def high_xT(g, j):
                act.wait_ge(xT_ps, tile_of(g, j) + 1)
                act.activation(xT_h[:, j % 2].rearrange("p c t -> p (c t)"), px[:], ACT.Copy).then_inc(xT_h_ok, 1)

            def high_u(g, j, half):
                act.wait_ge(u_ps[half], tile_of(g, j) + 1)
                act.activation(u_h[:, j, half, :], pu[half][:, 0:HC], ACT.Copy).then_inc(u_h_ok[half], 1)

            def exps(g, j):
                act.wait_ge(nmax_ok, tile_of(g, j) + 1)
                act.activation(eprob[:], small[:, R:SM], ACT.Exp, bias=nmax[:, 0:1],
                               accum_out=esum[:, 0:1]).then_inc(eprob_ok, 1)

            def high_zT(g, j):
                act.wait_ge(zT_ps, tile_of(g, j) + 1)
                act.activation(zT_h[:], pzT, ACT.Copy).then_inc(zT_h_ok, 1)

            def high_mT(g, j):
                act.wait_ge(mT_ps, tile_of(g, j) + 1)
                act.activation(tail_s[0:BIAS, j % 2, :], pmT, ACT.Copy).then_inc(mT_h_ok, 1)

            def high_w(k):
                act.wait_ge(wT_ps, k + 1)
                act.activation(WT_h[:, k, :, 0:OH], pm[k // 2][:, k % 2, :].rearrange("p (h o) -> p h o", h=2),
                               ACT.Copy).then_inc(wT_h_ok, 1)

            act.wait_ge(consts, 2)
            act.activation(gelu_one[:], ones_r[:, 0:1].bitcast(F32), ACT.Gelu)
            act.wait_ge(ld_b01, 32)
            act.wait_ge(h1_ps, 1)
            act.activation(h1T[:], pz[:, P:2 * P], ACT.Gelu, bias=b0_col[:, 0:1]).then_inc(h1_ok, 1)
            act.wait_ge(h2_ps, 1)
            act.activation(h2T[:], pz[:, 0:P], ACT.Gelu, bias=b1_col[:, 0:1]).then_inc(h2_ok, 1)
            high_xT(0, 0)
            act.wait_ge(cnmax_ok, 1)
            act.activation(cexp[:], clog[:], ACT.Exp, bias=cnmax[:, 0:1], accum_out=csum[:, 0:1]).then_inc(cexp_ok, 1)
            high_w(0)
            act.wait_ge(arT_ps, 1)
            act.activation(WT_h[:, :, :, OH:HC],
                           pu[1][:, 0:DC * SM].rearrange("p (c h s) -> p c h s", c=DC, h=2),
                           ACT.Copy).then_inc(arT_h_ok, 1)
            high_w(1)
            high_w(2)
            act.wait_ge(aggw_ps, 1)
            act.activation(aggw_sb[:, 0:IH, :].rearrange("b i o -> b (i o)"), pu[0][:], ACT.Copy).then_inc(aggw_a, 1)
            high_w(3)

            def biases():
                act.wait_ge(wsum_ps, 1)
                for r in range(0, 3, 2):
                    act.activation(row_src[0:1, r, :].rearrange("p (h o) -> p h o", h=2), pm[0][0:1, :, 0:OH],
                                   ACT.Copy).then_inc(row_h_ok, 1)
                act.wait_ge(ld_bb, 16)
                act.activation(row_src[0:1, 3, :], bb_row[:], ACT.Copy).then_inc(row_h_ok, 1)

            def low_rank_weights():
                act.wait_ge(bwT_ps, 1)
                act.wait_ge(consts, 2)
                for row in (MID_H, MID_L):
                    act.activation(tail_w[row:row + R, :], pm[1][0:R, 0, :], ACT.Copy,
                                   scale=SCALING).then_inc(bwT_h_ok, 1)
                act.wait_ge(ld_cores, 16)
                act.activation(core_h[:].rearrange("p (n c) -> p n c", n=3)[:, :, 0:R],
                               cores_sb[:].unsqueeze(1).to_broadcast([P, 3, R]), ACT.Copy).then_inc(core_h_ok, 1)

            def step(g, j):
                m, r = back(g, j, LAG), back(g, j, LAG + 1)
                if real(*r):
                    high_mT(*r)
                if real(*m):
                    exps(*m)
                if real(*ahead(g, j)):
                    high_xT(*ahead(g, j))
                if real(*m):
                    high_zT(*m)
                if real(g, j):
                    high_u(g, j, 0)
                if first(g, j, 0):
                    biases()
                if real(g, j):
                    high_u(g, j, 1)
                if first(g, j, 0):
                    low_rank_weights()

            run(act, step)

        @block.vector
        def _(dve):
            def low(out_, psum, high):
                return dve.tensor_tensor(out_, psum, high.bitcast(F32), ALU.subtract)

            def low_xT(g, j):
                dve.wait_ge(xT_h_ok, tile_of(g, j) + 1)
                low(xT_l[:, j % 2].rearrange("p c t -> p (c t)"), px[:],
                    xT_h[:, j % 2].rearrange("p c t -> p (c t)")).then_inc(xT_l_ok, 1)

            def low_u(g, j, half):
                dve.wait_ge(u_h_ok[half], tile_of(g, j) + 1)
                low(u_l[:, j, half, :], pu[half][:, 0:HC], u_h[:, j, half, :]).then_inc(u_l_ok[half], 1)

            def small_columns(g, j):
                m = tile_of(g, j)
                par = j % 2
                dve.wait_ge(mix_ps[par], nth_of_parity(g, j) + 1)
                wait_past(dve, z_ok, m)
                dve.scalar_tensor_tensor(out=small[:].rearrange("p (h s) -> p h s", h=2),
                                         in0=wsum_s[:].rearrange("p (h s) -> p h s", h=2),
                                         scalar=aggb_col[:, bass.ds(m, 1)],
                                         in1=pm[par][:, :, OH:HC],
                                         op0=ALU.mult, op1=ALU.add).then_inc(small_ok, 1)
                dve.wait_ge(small_ok, m + 1)
                dve.tensor_reduce(nmax[:], small[:, R:SM], AX_X, ALU.max, negate=True).then_inc(nmax_ok, 1)

            def routed(g, j):
                m = tile_of(g, j)
                dve.wait_ge(eprob_ok, m + 1)
                dve.reciprocal(rinv[:], esum[:]).then_inc(rinv_ok, 1)
                wait_past(dve, zT_ps, m)
                dve.wait_ge(rinv_ok, m + 1)
                dve.scalar_tensor_tensor(out=z[:], in0=small[:, 0:R].unsqueeze(1).to_broadcast([P, E, R]),
                                         scalar=rinv[:, 0:1], in1=eprob[:].unsqueeze(2).to_broadcast([P, E, R]),
                                         op0=ALU.mult, op1=ALU.mult).then_inc(z_ok, 1)

            def low_zT(g, j):
                dve.wait_ge(zT_h_ok, tile_of(g, j) + 1)
                low(zT_l[:], pzT, zT_h[:]).then_inc(zT_l_ok, 1)

            def low_mT(g, j):
                dve.wait_ge(mT_h_ok, tile_of(g, j) + 1)
                low(tail_s[MID_L:MID_L + R, j % 2, :], pz[MID_L:MID_L + R, P:2 * P],
                    tail_s[MID_L:MID_L + R, j % 2, :]).then_inc(mT_l_ok, 1)

            def final(g, j):
                par = j % 2
                dve.wait_ge(x_kept[j], 16 * (g + 1))
                wait_past(dve, stored[j], 16 * g)
                dve.wait_ge(tail_ps[par], nth_of_parity(g, j) + 1)
                dve.tensor_tensor(out_sb[:, j, :].rearrange("p (h o) -> p h o", h=2), pm[par][:, :, 0:OH],
                                  xres[:, j, :].rearrange("p (h o) -> p h o", h=2),
                                  ALU.add).then_inc(final_ok[par], 1)

            def low_w(k):
                dve.wait_ge(wT_h_ok, k + 1)
                low(WT_l[:, k, :, 0:OH], pm[k // 2][:, k % 2, :].rearrange("p (h o) -> p h o", h=2),
                    WT_h[:, k, :, 0:OH]).then_inc(wT_l_ok, 1)

            dve.memset(samemask[:], 0.0).then_inc(consts, 1)
            dve.memset(core_h[:].bitcast(F32), 0.0)
            dve.memset(core_l[:].bitcast(F32), 0.0)
            dve.memset(tail_w[:].bitcast(F32), 0.0)
            dve.memset(ones_r[:].bitcast(F32), 1.0).then_inc(consts, 1)
            dve.wait_ge(consts, 2)
            for s in range(SPT):
                dve.memset(samemask[s * CH:(s + 1) * CH, s:s + 1], 1.0).then_inc(consts, 1)
            dve.wait_ge(condT_ps, 1)
            dve.tensor_copy(condT[:], pz[:, 0:P]).then_inc(condT_ok, 1)
            dve.wait_ge(ld_b2, 16)
            dve.wait_ge(clog_ps, 1)
            dve.tensor_tensor(clog[:], pz[:, P:P + KC], b2_bc[:], ALU.add).then_inc(clog_ok, 1)
            dve.wait_ge(clog_ok, 1)
            dve.tensor_reduce(cnmax[:], clog[:], AX_X, ALU.max, negate=True).then_inc(cnmax_ok, 1)
            low_xT(0, 0)
            dve.wait_ge(cexp_ok, 1)
            dve.reciprocal(crinv[:], csum[:]).then_inc(crinv_ok, 1)
            dve.wait_ge(crinv_ok, 1)
            dve.tensor_scalar(att[:], cexp[:], crinv[:, 0:1], None, ALU.mult).then_inc(att_ok, 1)
            dve.wait_ge(attT_ps, 1)
            dve.tensor_copy(attT[:], pz[0:KC, 0:P]).then_inc(attT_ok, 1)
            low_w(0)
            dve.wait_ge(arT_h_ok, 1)
            low(WT_l[:, :, :, OH:HC], pu[1][:, 0:DC * SM].rearrange("p (c h s) -> p c h s", c=DC, h=2),
                WT_h[:, :, :, OH:HC]).then_inc(arT_l_ok, 1)
            low_w(1)
            low_w(2)
            dve.wait_ge(aggw_ps, 2)
            dve.tensor_copy(aggw_sb[:, IH:CH, :].rearrange("b i o -> b (i o)"), pu[1][:]).then_inc(aggw_d, 1)
            dve.wait_ge(aggb_ps, 1)
            dve.tensor_copy(aggb_hl[:, 0, :], pz[:, 0:CH]).then_inc(aggb_hl_ok, 1)
            dve.wait_ge(aggb_hl_ok, 1)
            low(aggb_hl[:, 1, :], pz[:, 0:CH], aggb_hl[:, 0, :]).then_inc(aggb_hl_ok, 1)
            low_w(3)
            for s in range(SPT):
                dve.tensor_copy(aggb_col[s * CH:(s + 1) * CH, :],
                                pz[s * CH:(s + 1) * CH, P:2 * P].rearrange("p (t s) -> p s t", s=SPT)[:, s, :]
                                ).then_inc(aggb_col_ok, 1)

            def biases():
                dve.wait_ge(row_h_ok, 2)
                low(row_src[0:1, 1, :].rearrange("p (h o) -> p h o", h=2), pm[0][0:1, :, 0:OH],
                    row_src[0:1, 0, :].rearrange("p (h o) -> p h o", h=2)).then_inc(row_l_ok, 1)
                dve.tensor_copy(wsum_s[:].rearrange("p (h s) -> p h s", h=2), pm[0][:, :, OH:HC]).then_inc(wsum_s_ok, 1)
                dve.wait_ge(row_h_ok, 3)
                low(row_src[0:1, 4, :], bb_row[:], row_src[0:1, 3, :]).then_inc(row_l_ok, 1)

            def low_rank_weights():
                dve.wait_ge(bwT_h_ok, 2)
                dve.scalar_tensor_tensor(out=tail_w[MID_H2:MID_H2 + R, :], in0=pm[1][0:R, 0, :], scalar=SCALING,
                                         in1=tail_w[MID_H:MID_H + R, :].bitcast(F32),
                                         op0=ALU.mult, op1=ALU.subtract).then_inc(bwT_l_ok, 1)
                dve.wait_ge(core_h_ok, 1)
                low(core_l[:, 0:R], cores_sb[:], core_h[:, 0:R])
                for row in (MID_L, MID_H2):
                    last = low(core_l[:, row:row + R], cores_sb[:], core_h[:, 0:R])
                last.then_inc(core_l_ok, 1)

            def step(g, j):
                before, m, r = back(g, j, 1), back(g, j, LAG), back(g, j, LAG + 1)
                if real(*r):
                    low_mT(*r)
                if first(g, j, LAG):
                    dve.wait_ge(wsum_s_ok, 1)
                    dve.wait_ge(aggb_col_ok, SPT)
                if real(*m):
                    small_columns(*m)
                if real(*before) and not first(g, j, 1):
                    low_u(*before, 1)
                if real(*m):
                    routed(*m)
                if real(*r):
                    final(*r)
                if real(*ahead(g, j)):
                    low_xT(*ahead(g, j))
                if real(*m):
                    low_zT(*m)
                if real(g, j):
                    low_u(g, j, 0)
                if first(g, j, 0):
                    biases()
                    low_u(0, 0, 1)
                    low_rank_weights()

            run(dve, step)


_INS = ['x', 'cond_128', 'L0_cond_W0', 'L0_cond_b0', 'L0_cond_W1', 'L0_cond_b1', 'L0_cond_W2', 'L0_cond_b2',
        'L0_cond_weight', 'L0_cond_bias_k', 'L0_ffn_W_base', 'L0_ffn_b_base', 'L0_ffn_A_w', 'L0_ffn_B_w',
        'L0_ffn_router_w', 'L0_ffn_cores']


def kernel(**inputs):
    import numpy as _np
    import concourse.bacc as _bacc
    from concourse import mybir as _mybir
    from concourse.bass_utils import run_bass_kernel_spmd as _run

    nc = _bacc.Bacc("TRN2", target_bir_lowering=False, num_devices=1)
    arrays, args = {}, []
    for name in _INS:
        a = _np.ascontiguousarray(inputs[name])
        arrays[f"in_{name}_dram"] = a
        args.append(nc.dram_tensor(f"in_{name}_dram", a.shape, _mybir.dt.from_np(a.dtype), kind="ExternalInput").ap())
    out = nc.dram_tensor("out_0_dram", inputs['x'].shape, _mybir.dt.float32, kind="ExternalOutput").ap()
    adaln_ffn(nc, *args, out)
    r = _run(nc, [arrays], core_ids=[0])
    return r.results[0]["out_0_dram"]
```

```python
from contextlib import ExitStack

import concourse.bass as bass
from concourse import mybir

F32 = mybir.dt.float32
F32R = mybir.dt.float32r
ALU = mybir.AluOpType
ACT = mybir.ActivationFunctionType
AX_X = mybir.AxisListType.X

P = 128
GROUP = 8
WARM = {"start": 9, "condT": 3, "h1": 2, "h2": 4, "clog": 9, "agg2": 4, "agg3": 4}


def adaln_ffn(nc, x, cond, W0, b0, W1, b1, W2, b2, weight, bias_k, W_base, b_base, A_w, B_w,
              router_w, cores, out):
    BATCH, CH, D = x.shape
    KC = W2.shape[1]
    O = W_base.shape[0]
    E, R, _ = cores.shape
    SPT = P // CH
    TILES = BATCH * CH // P
    GROUPS = TILES // GROUP
    DC = D // P
    OH = O // 2
    SM = R + E
    COLS = (OH + SM, OH)
    SCALING = 2.0
    KW, KB = KC * CH * CH // P, KC * CH // P
    AC = 8
    STACK = 3 * KC
    assert E * R == P and O % 2 == 0 and D % P == 0 and TILES % GROUP == 0 and BATCH == P
    HIGH, MIDDLE, LOW, BIAS = 0, 32, 64, 96
    YBUFS = 4
    NBIAS = 5

    x_t = x.rearrange("(g j s) c d -> g j (s c) d", j=GROUP, s=SPT)
    out_t = out.rearrange("(g j s) c d -> g j (s c) d", j=GROUP, s=SPT)

    with ExitStack() as ctx:
        def sb(name, shape, dt=F32):
            return ctx.enter_context(nc.sbuf_tensor(name, shape, dt))

        def ps(name, shape):
            return ctx.enter_context(nc.psum_tensor(name, shape, F32))

        def sem(name):
            return ctx.enter_context(nc.semaphore(name))

        ident = sb("ident", [P, P])
        one = sb("one", [P, 1])
        gelu_one = sb("gelu_one", [P, 1])
        cond_sb = sb("cond_sb", [P, P])
        condT = sb("condT", [P, P])
        W0_sb = sb("W0_sb", [P, P])
        W1_sb = sb("W1_sb", [P, P])
        W2_sb = sb("W2_sb", [P, KC])
        b0_col = sb("b0_col", [P, 1])
        b1_col = sb("b1_col", [P, 1])
        b2_bc = sb("b2_bc", [P, KC])
        h1T = sb("h1T", [P, P])
        h2T = sb("h2T", [P, P])
        clog = sb("clog", [P, KC])
        cnmax = sb("cnmax", [P, 1])
        cexp = sb("cexp", [P, KC])
        csum = sb("csum", [P, 1])
        crinv = sb("crinv", [P, 1])
        att = sb("att", [P, KC])
        att_h = sb("att_h", [P, KC], F32R)
        att3 = sb("att3", [P, 3, KC])
        attS = sb("attS", [STACK, P], F32R)
        kw = sb("kw", [P, KW])
        kw_h = sb("kw_h", [P, KW], F32R)
        kw_l = sb("kw_l", [P, KW], F32R)
        kb = sb("kb", [P, KB])
        kb_h = sb("kb_h", [P, KB], F32R)
        kb_l = sb("kb_l", [P, KB], F32R)
        kwS = sb("kwS", [STACK, CH + 1, CH], F32R)
        ablk = sb("ablk", [P, TILES, SPT, CH])
        aggb_hl = sb("aggb_hl", [P, 2, CH], F32R)
        aggb_col = sb("aggb_col", [P, TILES])
        bias_rows = sb("bias_rows", [P, TILES * P])
        Wb_sb = sb("Wb_sb", [P, O // P, D])
        ar_sb = sb("ar_sb", [SM, D])
        Bw_sb = sb("Bw_sb", [P, O // P, R])
        bb_row = sb("bb_row", [1, O])
        cores_sb = sb("cores_sb", [P, R])
        WT_h = sb("WT_h", [P, DC, 2, COLS[0]], F32R)
        WT_l = sb("WT_l", [P, DC, 2, COLS[0]], F32R)
        wsum_s = sb("wsum_s", [P, SM])
        wsum_parts = sb("wsum_parts", [P, O // P, DC])
        scrap = sb("scrap", [P, O // P, P])
        scrap_ar = sb("scrap_ar", [SM, D])
        wsum_col = sb("wsum_col", [P, O // P])
        wsum_a = sb("wsum_a", [SM, 1])
        wsum_hl = sb("wsum_hl", [O // P, 2, P], F32R)
        bb_hl = sb("bb_hl", [1, 2, O], F32R)
        core_h = sb("core_h", [P, BIAS], F32R)
        core_l = sb("core_l", [P, BIAS], F32R)
        tail_w = sb("tail_w", [P, O], F32R)
        x_sb = sb("x_sb", [P, GROUP, D])
        yT_h = sb("yT_h", [P, YBUFS, DC, P], F32R)
        yT_l = sb("yT_l", [P, YBUFS, DC, P], F32R)
        small = sb("small", [P, SM])
        nmax = sb("nmax", [P, 1])
        eprob = sb("eprob", [P, E])
        esum = sb("esum", [P, 1])
        rinv = sb("rinv", [P, 1])
        z = sb("z", [P, E, R])
        zT_h = sb("zT_h", [P, P], F32R)
        zT_l = sb("zT_l", [P, P], F32R)
        tail_s = sb("tail_s", [P, 2, P], F32R)
        out_sb = sb("out_sb", [P, GROUP, O])

        pm = [ps("pm0", [P, 2, 512]), ps("pm1", [P, 2, 512])]
        pq = ps("pq", [P, 2, 512])
        px = ps("px", [P, 512])
        pz = ps("pz", [P, 512])
        agg_banks = [pq[:], pm[1][:], pm[0][:], pq[:]]
        w_banks = [pm[0][:, 0], pm[0][:, 1], pm[1][:, 0], pm[1][:, 1]]
        arT = pz[:, P:P + DC * SM]
        bwT = pm[1][0:R, 1]
        wsumT = pm[1][0:O // P, 0, 0:P]
        wsum_bc = pz[:, 0:SM]

        def pm_of(g, j):
            return pq if last_tile(g, j) else pm[j % 2]

        def pzT(g, j):
            return (px if last_tile(g, j) else pz)[:, 0:P]

        def pmT(g, j):
            return (px if last_tile(g, j) else pz)[0:BIAS, P:2 * P]

        def yT_bank(g, j):
            return pq[:, 1] if is_tile(g, j, 1) else px[:]

        ld_cond, ld_w0, ld_w1, ld_w2 = sem("ld_cond"), sem("ld_w0"), sem("ld_w1"), sem("ld_w2")
        ld_b0, ld_b1, ld_b2, ld_kw, ld_kb = sem("ld_b0"), sem("ld_b1"), sem("ld_b2"), sem("ld_kw"), sem("ld_kb")
        ld_ar, ld_bw, ld_bb = sem("ld_ar"), sem("ld_bw"), sem("ld_bb")
        ld_wb = [sem(f"ld_wb{k}") for k in range(DC)]
        ld_cores = sem("ld_cores")
        ld_x = [sem(f"ld_x{j}") for j in range(GROUP)]
        stored = [sem(f"stored{j}") for j in range(GROUP)]
        rows_back = sem("rows_back")
        tail_rows = sem("tail_rows")
        one_set, zeros_set, ablk_zero_d, ablk_zero_p = (
            sem("one_set"), sem("zeros_set"), sem("ablk_zero_d"), sem("ablk_zero_p"))
        ident_ok, tail_s_set = sem("ident_ok"), sem("tail_s_set")
        condT_ps, condT_ok = sem("condT_ps"), sem("condT_ok")
        h1_ps, h1_ok, h2_ps, h2_ok = sem("h1_ps"), sem("h1_ok"), sem("h2_ps"), sem("h2_ok")
        clog_ps, clog_ok, cnmax_ok, cexp_ok = sem("clog_ps"), sem("clog_ok"), sem("cnmax_ok"), sem("cexp_ok")
        crinv_ok, att_ok, att3_ok, attT_ps, attS_ok = (
            sem("crinv_ok"), sem("att_ok"), sem("att3_ok"), sem("attT_ps"), sem("attS_ok"))
        kw_h_ok, kw_l_ok, kwS_back = sem("kw_h_ok"), sem("kw_l_ok"), sem("kwS_back")
        kb_h_ok, kb_l_ok, kbS_back = sem("kb_h_ok"), sem("kb_l_ok"), sem("kbS_back")
        aggw_ps, ablk_a, ablk_d = sem("aggw_ps"), sem("ablk_a"), sem("ablk_d")
        aggb_ps, aggb_hl_ok, aggb_col_ok = sem("aggb_ps"), sem("aggb_hl_ok"), sem("aggb_col_ok")
        arT_ps, arT_h_ok, arT_l_ok = sem("arT_ps"), sem("arT_h_ok"), sem("arT_l_ok")
        wT_ps, wT_h_ok, wT_l_ok = sem("wT_ps"), sem("wT_h_ok"), sem("wT_l_ok")
        wsum_parts_ok, wsum_last_ok, wsum_a_ok, wsum_col_ok, wsum_ps = (
            sem("wsum_parts_ok"), sem("wsum_last_ok"), sem("wsum_a_ok"), sem("wsum_col_ok"), sem("wsum_ps"))
        wsum_h_ok, wsum_l_ok, wsum_s_ok = sem("wsum_h_ok"), sem("wsum_l_ok"), sem("wsum_s_ok")
        bb_h_ok, bb_l_ok = sem("bb_h_ok"), sem("bb_l_ok")
        bwT_ps, bwT_h_ok, bwT_l_ok = sem("bwT_ps"), sem("bwT_h_ok"), sem("bwT_l_ok")
        core_h_ok, core_l_ok = sem("core_h_ok"), sem("core_l_ok")
        yT_ps, yT_h_ok = sem("yT_ps"), sem("yT_h_ok")
        yT_l_ok, y0_l_ok = sem("yT_l_ok"), sem("y0_l_ok")
        u_ps = sem("u_ps")
        small_ok, nmax_ok, eprob_ok, rinv_ok, z_ok = (
            sem("small_ok"), sem("nmax_ok"), sem("eprob_ok"), sem("rinv_ok"), sem("z_ok"))
        zT_ps, zT_h_ok, zT_l_ok = sem("zT_ps"), sem("zT_h_ok"), sem("zT_l_ok")
        mT_ps, mT_h_ok, mT_l_ok = sem("mT_ps"), sem("mT_h_ok"), sem("mT_l_ok")
        brow_ok = sem("brow_ok")
        tail_ps = [sem("tail_ps0"), sem("tail_ps1")]
        final_ok = [sem("final_ok0"), sem("final_ok1")]

        block = ctx.enter_context(nc.Block())

        def tile_of(g, j):
            return g * GROUP + j

        def nth_of_parity(g, j):
            return g * (GROUP // 2) + j // 2

        def wait_past(eng, semaphore, n):
            if not (isinstance(n, int) and n <= 0):
                eng.wait_ge(semaphore, n)

        def back(g, j, n):
            return (g, j - n) if j >= n else (g - 1, j - n + GROUP)

        def ahead(g, j, n):
            return (g, j + n) if j + n < GROUP else (g + 1, j + n - GROUP)

        def real(g, j):
            return not isinstance(g, int) or 0 <= tile_of(g, j) < TILES

        def is_tile(g, j, t):
            return isinstance(g, int) and tile_of(g, j) == t

        def first(g, j):
            return is_tile(g, j, 0)

        def last_tile(g, j):
            return is_tile(g, j, TILES - 1)

        def run(eng, step, closing=None):
            for j in range(GROUP):
                step(0, j)
            with eng.Fori(1, GROUPS - 1) as g:
                for j in range(GROUP):
                    step(g, j)
            for j in range(GROUP - 2 if closing else GROUP):
                step(GROUPS - 1, j)
            if closing:
                closing(*((GROUPS - 1, GROUP - n) for n in (3, 2, 1)))

        @block.sync
        def _(sp):
            def load_wb(k):
                sp.dma_start(Wb_sb[:, :, k * P:(k + 1) * P],
                             W_base[:, k * P:(k + 1) * P].rearrange("(c p) d -> p c d", p=P)).then_inc(ld_wb[k], 16)

            def stack_kw(n, part):
                sp.dma_start(kwS[n * KC:(n + 1) * KC, 0:CH, :].bitcast(F32),
                             part[:].bitcast(F32)).then_inc(kwS_back, 16)

            def stack_kb(n, part):
                sp.dma_start(kwS[n * KC:(n + 1) * KC, CH, :].bitcast(F32),
                             part[:].bitcast(F32)).then_inc(kbS_back, 16)

            def load_x(g, j):
                sp.dma_start(x_sb[:, j, :], x_t[g, j]).then_inc(ld_x[j], 16)

            sp.dma_start(cond_sb[:], cond).then_inc(ld_cond, 16)
            sp.dma_start(W0_sb[:], W0).then_inc(ld_w0, 16)
            sp.dma_start(kw[:], weight.rearrange("k (h o) i one -> (k h) (o i one)", h=P // KC)).then_inc(ld_kw, 16)
            sp.dma_start(W1_sb[:], W1).then_inc(ld_w1, 16)
            load_wb(0)
            sp.wait_ge(kw_h_ok, 1)
            stack_kw(0, kw_h)
            stack_kw(1, kw_h)
            sp.wait_ge(kw_l_ok, 1)
            stack_kw(2, kw_l)
            load_wb(1)
            load_wb(2)
            load_wb(3)
            load_x(0, 0)
            load_x(0, 1)
            sp.wait_ge(kb_h_ok, 1)
            stack_kb(0, kb_h)
            stack_kb(1, kb_h)
            sp.wait_ge(kb_l_ok, 1)
            stack_kb(2, kb_l)
            load_x(0, 2)
            load_x(0, 3)
            sp.wait_ge(aggb_hl_ok, 2)
            for r, part in enumerate((0, 1, 0)):
                sp.dma_start(bias_rows[BIAS + r:BIAS + r + 1, :],
                             aggb_hl[:, part, :].bitcast(F32)).then_inc(rows_back, 16)
            sp.wait_ge(zeros_set, 1)
            sp.wait_ge(bb_l_ok, 1)
            sp.dma_start(tail_w[BIAS + 3:BIAS + NBIAS, :].bitcast(F32),
                         bb_hl[:].rearrange("p r o -> p (r o)").bitcast(F32)).then_inc(tail_rows, 16)
            load_x(0, 4)
            sp.wait_ge(wsum_h_ok, 1)
            sp.wait_ge(wsum_l_ok, 1)
            for r, part in enumerate((0, 0, 1)):
                sp.dma_start(tail_w[BIAS + r:BIAS + r + 1, :].bitcast(F32),
                             wsum_hl[:, part, :].bitcast(F32)).then_inc(tail_rows, 16)
            for j in range(5, GROUP):
                load_x(0, j)

            def store(g, j):
                n = nth_of_parity(g, j)
                if last_tile(g, j):
                    for h in range(2):
                        cols = slice(h * OH, (h + 1) * OH)
                        sp.wait_ge(final_ok[j % 2], n + h + 1)
                        sp.dma_start(out_t[g, j][:, cols], out_sb[:, j, cols]).then_inc(stored[j], 16)
                else:
                    sp.wait_ge(final_ok[j % 2], n + 1)
                    sp.dma_start(out_t[g, j], out_sb[:, j, :]).then_inc(stored[j], 16)

            def step(g, j):
                if real(g, j):
                    store(g, j)
                    if real(g + 1, j):
                        sp.wait_ge(yT_ps, tile_of(g, j) + 1)
                        load_x(g + 1, j)

            run(sp, step)
            for j in range(GROUP):
                sp.wait_ge(stored[j], 16 * (GROUPS + (1 if j == GROUP - 1 else 0)))

        @block.gpsimd
        def _(pool):
            pool.memset(ident[:], 0.0).then_inc(ident_ok, 1)
            pool.wait_ge(ident_ok, 1)
            pool.affine_select(out=ident[:], in_=ident[:], compare_op=ALU.not_equal, fill=1.0, base=0,
                               pattern=[[-1, P]], channel_multiplier=1).then_inc(ident_ok, 1)
            pool.dma_start(b0_col[:], b0.unsqueeze(1)).then_inc(ld_b0, 16)
            pool.dma_start(b1_col[:], b1.unsqueeze(1)).then_inc(ld_b1, 16)
            pool.dma_start(W2_sb[:], W2).then_inc(ld_w2, 16)
            pool.dma_start(b2_bc[:], b2.unsqueeze(0).to_broadcast([P, KC])).then_inc(ld_b2, 16)
            pool.dma_start(kb[:], bias_k.rearrange("k (h o) -> (k h) o", h=P // KC)).then_inc(ld_kb, 16)
            pool.wait_ge(ident_ok, 2)
            pool.memset(ablk[:, TILES // 2:TILES], 0.0).then_inc(ablk_zero_p, 1)
            pool.dma_start(ar_sb[0:R, :], A_w).then_inc(ld_ar, 16)
            pool.dma_start(ar_sb[R:SM, :], router_w).then_inc(ld_ar, 16)
            pool.dma_start(Bw_sb[:], B_w.rearrange("(c p) r -> p c r", p=P)).then_inc(ld_bw, 16)
            pool.dma_start(bb_row[:], b_base.unsqueeze(0)).then_inc(ld_bb, 16)
            pool.dma_start(cores_sb[:], cores.rearrange("e r q -> (e r) q")).then_inc(ld_cores, 16)
            pool.wait_ge(ablk_zero_p, 1)
            pool.memset(core_h[:].bitcast(F32), 0.0)
            pool.memset(core_l[:].bitcast(F32), 0.0)
            pool.memset(tail_w[:].bitcast(F32), 0.0).then_inc(zeros_set, 1)
            pool.wait_ge(zeros_set, 1)
            pool.memset(tail_s[BIAS:P].bitcast(F32), 1.0).then_inc(tail_s_set, 1)
            pool.wait_ge(tail_s_set, 1)
            pool.wait_ge(ld_bb, 16)
            pool.tensor_copy(bb_hl[0:1, 0, :], bb_row[:]).then_inc(bb_h_ok, 1)
            pool.wait_ge(bb_h_ok, 1)
            pool.tensor_tensor(bb_hl[0:1, 1, :], bb_row[:], bb_hl[0:1, 0, :].bitcast(F32),
                               ALU.subtract).then_inc(bb_l_ok, 1)
            pool.wait_ge(bb_l_ok, 1)
            pool.wait_ge(rows_back, 16 * 3)

            def bias_rows_of(g, j):
                m = tile_of(g, j)
                par = j % 2
                wait_past(pool, brow_ok, m)
                wait_past(pool, tail_ps[par], 2 * nth_of_parity(g, j))
                pool.tensor_copy(tail_s[BIAS:BIAS + 3, par, :],
                                 bias_rows[BIAS:BIAS + 3, bass.ds(m * P, P)]).then_inc(brow_ok, 1)

            for j in range(GROUP):
                bias_rows_of(0, j)
            with pool.Fori(1, GROUPS) as g:
                for j in range(GROUP):
                    bias_rows_of(g, j)

        @block.tensor
        def _(pe):
            def mix(g, j):
                t = tile_of(g, j)
                pe.wait_ge(ld_x[j], 16 * (g + 1))
                if not is_tile(g, j, 1):
                    wait_past(pe, yT_l_ok, t - 1)
                moving = ablk[:, bass.ds(t, 1), :, :].rearrange("p t s o -> p (t s o)")
                for k in range(DC):
                    last = pe.matmul(yT_bank(g, j)[:, k * P:(k + 1) * P], x_sb[:, j, k * P:(k + 1) * P], moving,
                                     start=True, stop=True)
                last.then_inc(yT_ps, 1)

            def product(g, j, half, k0=0, k1=DC):
                par = j % 2
                if half == 0 and not last_tile(g, j):
                    wait_past(pe, final_ok[par], nth_of_parity(g, j))
                for k in range(k0, k1):
                    if first(g, j) and half == 0:
                        pe.wait_ge(y0_l_ok, k // (DC // 2) + 1)
                        pe.wait_ge(wT_l_ok, k + 1)
                    for n, (s, w) in enumerate(((yT_h, WT_h), (yT_h, WT_l), (yT_l, WT_h))):
                        last = pe.matmul(pm_of(g, j)[:, half, 0:COLS[half]], s[:, j % YBUFS, k, :],
                                         w[:, k, half, 0:COLS[half]],
                                         start=(k == 0 and n == 0), stop=(k == DC - 1 and n == 2))
                if half == 0:
                    last.then_inc(u_ps, 1)

            def z_transpose(g, j):
                m = tile_of(g, j)
                pe.wait_ge(z_ok, m + 1)
                pe.transpose(pzT(g, j), z[:].rearrange("p e r -> p (e r)"), ident[:]).then_inc(zT_ps, 1)

            def core_product(g, j):
                pe.wait_ge(zT_l_ok, tile_of(g, j) + 1)
                for n, (s, w) in enumerate(((core_h, zT_h), (core_h, zT_l), (core_l, zT_h))):
                    last = pe.matmul(pmT(g, j), s[:], w[:], start=(n == 0), stop=(n == 2))
                last.then_inc(mT_ps, 1)

            def tail(g, j):
                m = tile_of(g, j)
                par = j % 2
                pe.wait_ge(mT_l_ok, m + 1)
                for half in range(2):
                    pe.matmul(pm_of(g, j)[:, half, 0:OH], tail_s[:, par, :],
                              tail_w[:, half * OH:(half + 1) * OH],
                              start=False, stop=True, skip_group_check=True).then_inc(tail_ps[par], 1)

            def keep_busy(n, bank=pq[:, 0]):
                for _ in range(n):
                    pe.transpose(bank[:, 0:P], ident[:], ident[:])

            def transposes_w(k):
                pe.wait_ge(ld_wb[k], 16)
                for c in range(O // P):
                    last = pe.transpose(w_banks[k][:, c * P:(c + 1) * P],
                                        Wb_sb[:, c, k * P:(k + 1) * P], ident[:])
                last.then_inc(wT_ps, 1)

            pe.wait_ge(ident_ok, 2)
            keep_busy(WARM["start"])
            pe.wait_ge(ld_cond, 16)
            pe.transpose(pz[:, 0:P], cond_sb[:], ident[:]).then_inc(condT_ps, 1)
            keep_busy(WARM["condT"])
            pe.wait_ge(ld_w0, 16)
            pe.wait_ge(condT_ok, 1)
            pe.matmul(pz[:, P:2 * P], W0_sb[:], condT[:], start=True, stop=True).then_inc(h1_ps, 1)
            keep_busy(WARM["h1"])
            pe.wait_ge(ld_w1, 16)
            pe.wait_ge(h1_ok, 1)
            pe.matmul(pz[:, 0:P], W1_sb[:], h1T[:], start=True, stop=True).then_inc(h2_ps, 1)
            keep_busy(WARM["h2"])
            pe.wait_ge(ld_w2, 16)
            pe.wait_ge(h2_ok, 1)
            pe.matmul(pz[:, P:P + KC], h2T[:], W2_sb[:], start=True, stop=True).then_inc(clog_ps, 1)
            transposes_w(0)
            keep_busy(WARM["clog"])
            pe.wait_ge(att3_ok, 2)
            pe.transpose(pz[0:STACK, 0:P], att3[:].rearrange("p n k -> p (n k)"), ident[:]).then_inc(attT_ps, 1)
            transposes_w(1)
            pe.wait_ge(kwS_back, 16 * 3)
            pe.wait_ge(attS_ok, 1)
            for n, banks in enumerate(agg_banks):
                if n == 2:
                    keep_busy(WARM["agg2"], px)
                    pe.wait_ge(wT_l_ok, 2)
                if n == 3:
                    keep_busy(WARM["agg3"], px)
                    pe.wait_ge(ablk_a, 1)
                for c in range(AC):
                    last = pe.matmul(banks[0:CH, c // 4, (c % 4) * P:(c % 4 + 1) * P], kwS[:, n * AC + c, :], attS[:],
                                     start=True, stop=True)
                last.then_inc(aggw_ps, 1)
            pe.wait_ge(ablk_d, 1)
            transposes_w(2)
            transposes_w(3)
            pe.wait_ge(ld_ar, 32)
            for k in range(DC):
                last = pe.transpose(arT[:, k * SM:(k + 1) * SM], ar_sb[:, k * P:(k + 1) * P], ident[0:SM, 0:SM])
            last.then_inc(arT_ps, 1)
            pe.wait_ge(ablk_a, 3)
            pe.wait_ge(ablk_d, 2)
            mix(0, 0)
            mix(0, 1)
            pe.wait_ge(arT_l_ok, 1)
            pe.wait_ge(kbS_back, 16 * 3)
            pe.matmul(pz[:, 2 * P:2 * P + CH], attS[:], kwS[:, CH, :], start=True, stop=True)
            pe.matmul(pz[0:CH, 3 * P:4 * P], kwS[:, CH, :], attS[:], start=True, stop=True)
            pe.wait_ge(wsum_a_ok, 1)
            pe.matmul(wsum_bc, wsum_a[:].to_broadcast([SM, P]), ident[0:SM, 0:SM],
                      start=True, stop=True).then_inc(aggb_ps, 1)

            def transposes_bw():
                pe.wait_ge(ld_bw, 16)
                for c in range(O // P):
                    last = pe.transpose(bwT[:, c * P:(c + 1) * P], Bw_sb[:, c, :], ident[:])
                last.then_inc(bwT_ps, 1)

            def column_sums():
                pe.wait_ge(wsum_col_ok, 1)
                pe.transpose(wsumT, wsum_col[:], ident[:]).then_inc(wsum_ps, 1)

            def step(g, j):
                r = back(g, j, 1)
                if first(*r):
                    pe.wait_ge(wsum_l_ok, 1)
                    pe.wait_ge(yT_l_ok, 1)
                product(g, j, 0)
                if first(g, j):
                    transposes_bw()
                if first(*r):
                    pe.wait_ge(core_l_ok, 1)
                if real(*r):
                    core_product(*r)
                mix(*ahead(g, j, 2))
                if first(g, j):
                    column_sums()
                if first(*r):
                    pe.wait_ge(tail_rows, 64)
                if first(*r):
                    pe.wait_ge(bwT_l_ok, 1)
                product(g, j, 1, 0, 1)
                if real(*r):
                    tail(*r)
                product(g, j, 1, 1, DC)
                if first(g, j):
                    pe.wait_ge(aggb_col_ok, SPT)
                z_transpose(g, j)

            def closing(y, a, b):
                product(*a, 0)
                core_product(*y)
                product(*b, 0)
                tail(*y)
                z_transpose(*a)
                product(*a, 1)
                core_product(*a)
                z_transpose(*b)
                product(*b, 1, 0, DC // 2)
                tail(*a)
                core_product(*b)
                product(*b, 1, DC // 2, DC)
                tail(*b)

            run(pe, step, closing)

        @block.scalar
        def _(act):
            def high_yT(g, j):
                act.wait_ge(yT_ps, tile_of(g, j) + 1)
                act.activation(yT_h[:, j % YBUFS].rearrange("p c t -> p (c t)"), yT_bank(g, j),
                               ACT.Copy).then_inc(yT_h_ok, 1)

            def exps(g, j):
                act.wait_ge(nmax_ok, tile_of(g, j) + 1)
                act.activation(eprob[:], small[:, R:SM], ACT.Exp, bias=nmax[:, 0:1],
                               accum_out=esum[:, 0:1]).then_inc(eprob_ok, 1)

            def high_zT(g, j):
                act.wait_ge(zT_ps, tile_of(g, j) + 1)
                act.activation(zT_h[:], pzT(g, j), ACT.Copy).then_inc(zT_h_ok, 1)

            def high_mT(g, j):
                act.wait_ge(mT_ps, tile_of(g, j) + 1)
                wait_past(act, tail_ps[j % 2], 2 * nth_of_parity(g, j))
                act.activation(tail_s[0:BIAS, j % 2, :], pmT(g, j), ACT.Copy).then_inc(mT_h_ok, 1)

            def high_w(k):
                act.wait_ge(wT_ps, k + 1)
                act.activation(WT_h[:, k, :, 0:OH], w_banks[k].rearrange("p (h o) -> p h o", h=2),
                               ACT.Copy).then_inc(wT_h_ok, 1)

            def block_diagonal(n, b0=0, b1=2):
                act.wait_ge(aggw_ps, n + 1)
                c0, c1 = n * AC + b0 * AC // 2, n * AC + b1 * AC // 2
                from_ps = agg_banks[n][0:CH, b0:b1].rearrange("p b (c t s) -> p t (b c) s", c=AC // 2, s=SPT)
                for s in range(SPT):
                    last = act.activation(ablk[s * CH:(s + 1) * CH, :, s, c0:c1], from_ps[:, :, :, s],
                                          ACT.Copy)
                last.then_inc(ablk_a, 1)

            act.wait_ge(one_set, 1)
            act.activation(gelu_one[:], one[:], ACT.Gelu)
            act.wait_ge(ld_b0, 16)
            act.wait_ge(h1_ps, 1)
            act.activation(h1T[:], pz[:, P:2 * P], ACT.Gelu, bias=b0_col[:, 0:1]).then_inc(h1_ok, 1)
            act.wait_ge(ld_b1, 16)
            act.wait_ge(h2_ps, 1)
            act.activation(h2T[:], pz[:, 0:P], ACT.Gelu, bias=b1_col[:, 0:1]).then_inc(h2_ok, 1)
            act.wait_ge(cnmax_ok, 1)
            act.activation(cexp[:], clog[:], ACT.Exp, bias=cnmax[:, 0:1], accum_out=csum[:, 0:1]).then_inc(cexp_ok, 1)
            high_w(0)
            act.wait_ge(attT_ps, 1)
            act.activation(attS[:], pz[0:STACK, 0:P], ACT.Copy).then_inc(attS_ok, 1)
            high_w(1)
            act.wait_ge(ablk_zero_d, 1)
            act.wait_ge(ablk_zero_p, 1)
            block_diagonal(0)
            block_diagonal(2)
            block_diagonal(3, 0, 1)
            high_w(2)
            high_w(3)
            act.wait_ge(arT_ps, 1)
            act.activation(WT_h[:, :, 0, OH:OH + SM], arT.rearrange("p (c s) -> p c s", c=DC),
                           ACT.Copy).then_inc(arT_h_ok, 1)
            act.activation(scrap_ar[:], ar_sb[:], ACT.Copy,
                           accum_out=wsum_a[:, 0:1]).then_inc(wsum_a_ok, 1)
            high_yT(0, 0)
            high_yT(0, 1)
            act.wait_ge(ld_wb[DC - 1], 16)
            for c in range(O // P):
                act.activation(scrap[:, c, :], Wb_sb[:, c, (DC - 1) * P:DC * P], ACT.Copy,
                               accum_out=wsum_parts[:, c, DC - 1:DC]).then_inc(wsum_last_ok, 1)

            def low_rank_weights():
                act.wait_ge(bwT_ps, 1)
                act.wait_ge(zeros_set, 1)
                for row in (HIGH, MIDDLE):
                    act.activation(tail_w[row:row + R, :], bwT, ACT.Copy,
                                   scale=SCALING).then_inc(bwT_h_ok, 1)
                act.wait_ge(ld_cores, 16)
                act.activation(core_h[:].rearrange("p (n c) -> p n c", n=3)[:, :, 0:R],
                               cores_sb[:].unsqueeze(1).to_broadcast([P, 3, R]), ACT.Copy).then_inc(core_h_ok, 1)

            def step(g, j):
                r = back(g, j, 1)
                if real(*r):
                    high_zT(*r)
                    high_mT(*r)
                exps(g, j)
                if first(g, j):
                    act.wait_ge(wsum_ps, 1)
                    act.activation(wsum_hl[:, 0, :], wsumT, ACT.Copy).then_inc(wsum_h_ok, 1)
                high_yT(*ahead(g, j, 2))
                if first(g, j):
                    low_rank_weights()

            def closing(y, a, b):
                high_zT(*y)
                high_mT(*y)
                exps(*a)
                high_zT(*a)
                exps(*b)
                high_mT(*a)
                high_zT(*b)
                high_mT(*b)

            run(act, step, closing)

        @block.vector
        def _(dve):
            def low(out_, whole, high):
                return dve.tensor_tensor(out_, whole, high.bitcast(F32), ALU.subtract)

            def low_yT(g, j):
                dve.wait_ge(yT_h_ok, tile_of(g, j) + 1)
                low(yT_l[:, j % YBUFS].rearrange("p c t -> p (c t)"), yT_bank(g, j),
                    yT_h[:, j % YBUFS].rearrange("p c t -> p (c t)")).then_inc(yT_l_ok, 1)

            def small_columns(g, j):
                m = tile_of(g, j)
                wait_past(dve, z_ok, m)
                dve.wait_ge(u_ps, m + 1)
                dve.scalar_tensor_tensor(out=small[:], in0=wsum_s[:], scalar=aggb_col[:, bass.ds(m, 1)],
                                         in1=pm_of(g, j)[:, 0, OH:OH + SM],
                                         op0=ALU.mult, op1=ALU.add).then_inc(small_ok, 1)
                dve.wait_ge(small_ok, m + 1)
                dve.tensor_reduce(nmax[:], small[:, R:SM], AX_X, ALU.max, negate=True).then_inc(nmax_ok, 1)

            def routed(g, j):
                m = tile_of(g, j)
                dve.wait_ge(eprob_ok, m + 1)
                dve.reciprocal(rinv[:], esum[:]).then_inc(rinv_ok, 1)
                wait_past(dve, zT_ps, m)
                dve.wait_ge(rinv_ok, m + 1)
                dve.scalar_tensor_tensor(out=z[:], in0=small[:, 0:R].unsqueeze(1).to_broadcast([P, E, R]),
                                         scalar=rinv[:, 0:1], in1=eprob[:].unsqueeze(2).to_broadcast([P, E, R]),
                                         op0=ALU.mult, op1=ALU.mult).then_inc(z_ok, 1)

            def low_zT(g, j):
                dve.wait_ge(zT_h_ok, tile_of(g, j) + 1)
                low(zT_l[:], pzT(g, j), zT_h[:]).then_inc(zT_l_ok, 1)

            def low_mT(g, j):
                dve.wait_ge(brow_ok, tile_of(g, j) + 1)
                dve.wait_ge(mT_h_ok, tile_of(g, j) + 1)
                low(tail_s[MIDDLE:MIDDLE + R, j % 2, :], pmT(g, j)[MIDDLE:MIDDLE + R, :],
                    tail_s[MIDDLE:MIDDLE + R, j % 2, :]).then_inc(mT_l_ok, 1)

            def final(g, j):
                par = j % 2
                n = nth_of_parity(g, j)
                wait_past(dve, stored[j], 16 * g)
                if last_tile(g, j):
                    for h in range(2):
                        cols = slice(h * OH, (h + 1) * OH)
                        dve.wait_ge(tail_ps[par], 2 * n + h + 1)
                        dve.tensor_tensor(out_sb[:, j, cols], pm_of(g, j)[:, h, 0:OH], x_sb[:, j, cols],
                                          ALU.add).then_inc(final_ok[par], 1)
                else:
                    dve.wait_ge(tail_ps[par], 2 * (n + 1))
                    dve.tensor_tensor(out_sb[:, j, :].rearrange("p (h o) -> p h o", h=2), pm_of(g, j)[:, :, 0:OH],
                                      x_sb[:, j, :].rearrange("p (h o) -> p h o", h=2),
                                      ALU.add).then_inc(final_ok[par], 1)

            def low_w(k):
                dve.wait_ge(wT_h_ok, k + 1)
                low(WT_l[:, k, :, 0:OH], w_banks[k].rearrange("p (h o) -> p h o", h=2),
                    WT_h[:, k, :, 0:OH]).then_inc(wT_l_ok, 1)

            def sum_w(k):
                dve.wait_ge(ld_wb[k], 16)
                dve.tensor_reduce(wsum_parts[:, :, k], Wb_sb[:, :, k * P:(k + 1) * P], AX_X,
                                  ALU.add).then_inc(wsum_parts_ok, 1)

            def block_diagonal(n, b0=0, b1=2):
                dve.wait_ge(aggw_ps, n + 1)
                c0, c1 = n * AC + b0 * AC // 2, n * AC + b1 * AC // 2
                from_ps = agg_banks[n][0:CH, b0:b1].rearrange("p b (c t s) -> p t (b c) s", c=AC // 2, s=SPT)
                for s in range(SPT):
                    last = dve.tensor_copy(ablk[s * CH:(s + 1) * CH, :, s, c0:c1], from_ps[:, :, :, s])
                last.then_inc(ablk_d, 1)

            dve.memset(one[:], 1.0).then_inc(one_set, 1)
            dve.memset(ablk[:, 0:TILES // 2], 0.0).then_inc(ablk_zero_d, 1)
            dve.wait_ge(condT_ps, 1)
            dve.tensor_copy(condT[:], pz[:, 0:P]).then_inc(condT_ok, 1)
            dve.wait_ge(ld_kw, 16)
            dve.tensor_copy(kw_h[:], kw[:]).then_inc(kw_h_ok, 1)
            dve.wait_ge(kw_h_ok, 1)
            low(kw_l[:], kw[:], kw_h[:]).then_inc(kw_l_ok, 1)
            sum_w(0)
            dve.wait_ge(ld_b2, 16)
            dve.wait_ge(clog_ps, 1)
            dve.tensor_tensor(clog[:], pz[:, P:P + KC], b2_bc[:], ALU.add).then_inc(clog_ok, 1)
            dve.wait_ge(clog_ok, 1)
            dve.tensor_reduce(cnmax[:], clog[:], AX_X, ALU.max, negate=True).then_inc(cnmax_ok, 1)
            dve.wait_ge(cexp_ok, 1)
            dve.reciprocal(crinv[:], csum[:]).then_inc(crinv_ok, 1)
            dve.wait_ge(crinv_ok, 1)
            dve.tensor_scalar(att_h[:], cexp[:], crinv[:, 0:1], None, ALU.mult).then_inc(att_ok, 1)
            dve.tensor_scalar(att[:], cexp[:], crinv[:, 0:1], None, ALU.mult).then_inc(att_ok, 1)
            dve.wait_ge(att_ok, 2)
            dve.tensor_copy(att3[:, 0::2, :], att_h[:].bitcast(F32).unsqueeze(1).to_broadcast([P, 2, KC])
                            ).then_inc(att3_ok, 1)
            low(att3[:, 1, :], att[:], att_h[:]).then_inc(att3_ok, 1)
            low_w(0)
            dve.wait_ge(ld_kb, 16)
            dve.tensor_copy(kb_h[:], kb[:]).then_inc(kb_h_ok, 1)
            dve.wait_ge(kb_h_ok, 1)
            low(kb_l[:], kb[:], kb_h[:]).then_inc(kb_l_ok, 1)
            sum_w(1)
            low_w(1)
            dve.wait_ge(ablk_zero_d, 1)
            dve.wait_ge(ablk_zero_p, 1)
            block_diagonal(1)
            sum_w(2)
            block_diagonal(3, 1, 2)
            low_w(2)
            low_w(3)
            dve.wait_ge(arT_h_ok, 1)
            low(WT_l[:, :, 0, OH:OH + SM], arT.rearrange("p (c s) -> p c s", c=DC),
                WT_h[:, :, 0, OH:OH + SM]).then_inc(arT_l_ok, 1)
            dve.wait_ge(yT_h_ok, 1)
            for c in (0, DC // 2):
                low(yT_l[:, 0, c:c + DC // 2].rearrange("p c t -> p (c t)"), px[:, c * P:(c + DC // 2) * P],
                    yT_h[:, 0, c:c + DC // 2].rearrange("p c t -> p (c t)")).then_inc(y0_l_ok, 1)
            dve.wait_ge(aggb_ps, 1)
            dve.tensor_copy(aggb_hl[:, 0, :], pz[:, 2 * P:2 * P + CH]).then_inc(aggb_hl_ok, 1)
            dve.wait_ge(aggb_hl_ok, 1)
            low(aggb_hl[:, 1, :], pz[:, 2 * P:2 * P + CH], aggb_hl[:, 0, :]).then_inc(aggb_hl_ok, 1)
            for s in range(SPT):
                dve.tensor_copy(aggb_col[s * CH:(s + 1) * CH, :],
                                pz[0:CH, 3 * P:4 * P].rearrange("p (t s) -> p s t", s=SPT)[:, s, :]
                                ).then_inc(aggb_col_ok, 1)
            dve.tensor_copy(wsum_s[:], wsum_bc).then_inc(wsum_s_ok, 1)
            low_yT(0, 1)
            dve.wait_ge(wsum_parts_ok, DC - 1)
            dve.wait_ge(wsum_last_ok, O // P)
            dve.tensor_reduce(wsum_col[:], wsum_parts[:], AX_X, ALU.add).then_inc(wsum_col_ok, 1)
            dve.wait_ge(wsum_s_ok, 1)
            dve.wait_ge(aggb_col_ok, SPT)

            def low_rank_weights():
                dve.wait_ge(bwT_h_ok, 2)
                dve.scalar_tensor_tensor(out=tail_w[LOW:LOW + R, :], in0=bwT, scalar=SCALING,
                                         in1=tail_w[HIGH:HIGH + R, :].bitcast(F32),
                                         op0=ALU.mult, op1=ALU.subtract).then_inc(bwT_l_ok, 1)
                dve.wait_ge(core_h_ok, 1)
                low(core_l[:, 0:R], cores_sb[:], core_h[:, 0:R])
                for row in (MIDDLE, LOW):
                    last = low(core_l[:, row:row + R], cores_sb[:], core_h[:, 0:R])
                last.then_inc(core_l_ok, 1)

            def step(g, j):
                r = back(g, j, 1)
                if real(*r):
                    low_zT(*r)
                small_columns(g, j)
                if real(*r):
                    low_mT(*r)
                if first(g, j):
                    dve.wait_ge(wsum_h_ok, 1)
                    low(wsum_hl[:, 1, :], wsumT, wsum_hl[:, 0, :]).then_inc(wsum_l_ok, 1)
                routed(g, j)
                if real(*r):
                    final(*r)
                low_yT(*ahead(g, j, 2))
                if first(g, j):
                    low_rank_weights()

            def closing(y, a, b):
                low_zT(*y)
                small_columns(*a)
                low_mT(*y)
                routed(*a)
                small_columns(*b)
                low_zT(*a)
                routed(*b)
                final(*y)
                low_mT(*a)
                low_zT(*b)
                final(*a)
                low_mT(*b)
                final(*b)

            run(dve, step, closing)


_INS = ['x', 'cond_128', 'L0_cond_W0', 'L0_cond_b0', 'L0_cond_W1', 'L0_cond_b1', 'L0_cond_W2', 'L0_cond_b2',
        'L0_cond_weight', 'L0_cond_bias_k', 'L0_ffn_W_base', 'L0_ffn_b_base', 'L0_ffn_A_w', 'L0_ffn_B_w',
        'L0_ffn_router_w', 'L0_ffn_cores']


def kernel(**inputs):
    import numpy as _np
    import concourse.bacc as _bacc
    from concourse import mybir as _mybir
    from concourse.bass_utils import run_bass_kernel_spmd as _run

    nc = _bacc.Bacc("TRN2", target_bir_lowering=False, num_devices=1)
    arrays, args = {}, []
    for name in _INS:
        a = _np.ascontiguousarray(inputs[name])
        arrays[f"in_{name}_dram"] = a
        args.append(nc.dram_tensor(f"in_{name}_dram", a.shape, _mybir.dt.from_np(a.dtype), kind="ExternalInput").ap())
    out = nc.dram_tensor("out_0_dram", inputs['x'].shape, _mybir.dt.float32, kind="ExternalOutput").ap()
    adaln_ffn(nc, *args, out)
    r = _run(nc, [arrays], core_ids=[0])
    return r.results[0]["out_0_dram"]
```
